# Optimizing a Trainium2 kernel written in Bass

```python
import numpy as np
import jax
import jax.numpy as jnp

def _softmax(x, axis=-1):
    return jax.nn.softmax(x, axis=axis)

def _gelu(x):
    return jax.nn.gelu(x, approximate=True)

def _silu(x):
    return jax.nn.silu(x)

def _sigmoid(x):
    return jax.nn.sigmoid(x)

def _layernorm(x, axis=-1, eps=1e-05):
    m = jnp.mean(x, axis=axis, keepdims=True)
    v = jnp.var(x, axis=axis, keepdims=True)
    return (x - m) / jnp.sqrt(v + eps)

def _scatter_add(tgt, idx, src, axis=0):
    return tgt.at[idx].add(src)

def _segment_sum(src, seg, n):
    return jax.ops.segment_sum(src, seg, n)
kernel_name = 'mk_gnn_preln_d2_gnn_r64_66c376'

def setup_inputs(seed: int=0):
    np.random.seed(seed)
    _w = jnp.asarray

    def _rec_inputs():
        import jax
        import jax.numpy as jnp
        _gk = jax.random.key(seed)
        x = -0.0001006 + 1 * jax.random.normal(jax.random.fold_in(_gk, 1), (100000, 48), jnp.float32)
        src = jax.random.randint(jax.random.fold_in(_gk, 2), (25000,), 0, 100000, jnp.int32)
        dst = jnp.minimum((100000 * jax.random.uniform(jax.random.fold_in(_gk, 3), (25000,)) ** 2.0).astype(jnp.int32), 99999)
        _o = jnp.argsort(dst, stable=True)
        src = src[_o]
        dst = dst[_o]
        edge_attr_32 = 0.000189758 + 1.00013 * jax.random.normal(jax.random.fold_in(_gk, 12), (25000, 32), jnp.float32)
        edge_weight = jax.random.uniform(jax.random.fold_in(_gk, 14), (25000,), jnp.float32, 0.0, 0.999998)
        return (x, src, dst, edge_attr_32, edge_weight)
    x, src, dst, edge_attr_32, edge_weight = _rec_inputs()

    def _L0_gnn_setup():
        import jax, jax.numpy as jnp
        import numpy as np
        N_NODES = 100000
        N_EDGES = 25000
        D_IN = 48
        D_OUT = 48
        key = jax.random.key(seed)
        k1, k2, k3, k4, k5 = jax.random.split(key, 5)
        x = jax.random.normal(k1, (N_NODES, D_IN), dtype=jnp.float32)
        init_range = np.sqrt(6.0 / (D_IN + D_OUT)).astype(np.float32)
        w = jax.random.uniform(k2, (D_IN, D_OUT), dtype=jnp.float32, minval=-init_range, maxval=init_range)
        b = jnp.zeros((D_OUT,), dtype=jnp.float32)
        edge_src = jax.random.randint(k3, (N_EDGES,), 0, N_NODES, dtype=jnp.int32)
        edge_dst = jax.random.randint(k4, (N_EDGES,), 0, N_NODES, dtype=jnp.int32)
        adj_vals = jax.random.uniform(k5, (N_EDGES,), dtype=jnp.float32)
        return {'x': x, 'w': w, 'b': b, 'edge_src': edge_src, 'edge_dst': edge_dst, 'adj_vals': adj_vals}
    _L0_gnn_all = _L0_gnn_setup()
    _L0_gnn_in = {k: v for k, v in _L0_gnn_all.items() if k in ('w', 'b')}
    del _L0_gnn_all

    def _L1_gnn_setup():
        import jax, jax.numpy as jnp
        import numpy as np
        N_NODES = 100000
        key = jax.random.key(seed)
        k1, k2, k3, k4, k5, k6 = jax.random.split(key, 6)
        node_dim, edge_dim, hidden = (48, 32, 128)
        E = 25000
        x = jax.random.normal(k1, (N_NODES, node_dim), dtype=jnp.float32)
        edge_index = jax.random.randint(k2, (2, E), 0, N_NODES, dtype=jnp.int64)
        edge_attr = jax.random.normal(k3, (E, edge_dim), dtype=jnp.float32)
        in_dim = 2 * node_dim + edge_dim
        s1 = 1.0 / np.sqrt(in_dim)
        s2 = 1.0 / np.sqrt(hidden)
        W1 = jax.random.uniform(k4, (in_dim, hidden), minval=-s1, maxval=s1, dtype=jnp.float32)
        b1 = jax.random.uniform(k5, (hidden,), minval=-s1, maxval=s1, dtype=jnp.float32)
        W2 = jax.random.uniform(k6, (hidden, node_dim), minval=-s2, maxval=s2, dtype=jnp.float32)
        b2 = jnp.zeros((node_dim,), dtype=jnp.float32)
        return {'x': x, 'edge_index': edge_index, 'edge_attr': edge_attr, 'W1': W1, 'b1': b1, 'W2': W2, 'b2': b2}
    _L1_gnn_all = _L1_gnn_setup()
    _L1_gnn_in = {k: v for k, v in _L1_gnn_all.items() if k in ('W1', 'b1', 'W2', 'b2')}
    del _L1_gnn_all
    return {'x': x, 'src': src, 'dst': dst, 'edge_attr_32': edge_attr_32, 'edge_weight': edge_weight, 'L0_gnn_w': _L0_gnn_in['w'], 'L0_gnn_b': _L0_gnn_in['b'], 'L1_gnn_W1': _L1_gnn_in['W1'], 'L1_gnn_b1': _L1_gnn_in['b1'], 'L1_gnn_W2': _L1_gnn_in['W2'], 'L1_gnn_b2': _L1_gnn_in['b2']}

def reference(x, src, dst, edge_attr_32, edge_weight, L0_gnn_w, L0_gnn_b, L1_gnn_W1, L1_gnn_b1, L1_gnn_W2, L1_gnn_b2):
    import jax
    import jax.numpy as jnp

    def _L0_gnn_ref(x, w, b, edge_src, edge_dst, adj_vals):
        import jax, jax.numpy as jnp
        import numpy as np
        N_NODES = 100000
        N_EDGES = 25000
        D_IN = 48
        D_OUT = 48
        xw = jnp.matmul(x, w)
        msgs = adj_vals[:, None] * xw[edge_src]
        agg = jax.ops.segment_sum(msgs, edge_dst, num_segments=N_NODES)
        return jax.nn.relu(agg + b)

    def _L1_gnn_ref(x, edge_index, edge_attr, W1, b1, W2, b2):
        import jax, jax.numpy as jnp
        import numpy as np
        N_NODES = 100000
        src, dst = (edge_index[0], edge_index[1])
        x_i = x[dst]
        x_j = x[src]
        tmp = jnp.concatenate([x_i, x_j, edge_attr], axis=1)
        h = jax.nn.relu(tmp @ W1 + b1)
        msg = h @ W2 + b2
        out = jax.ops.segment_sum(msg, dst, num_segments=N_NODES)
        return out
    edge_index = jnp.stack([src, dst])
    h = jnp.maximum(_layernorm(x, axis=-1), 0.0)
    x = x + _L0_gnn_ref(h, L0_gnn_w, L0_gnn_b, src, dst, edge_weight)
    h = jnp.maximum(_layernorm(x, axis=-1), 0.0)
    x = x + _L1_gnn_ref(h, edge_index, edge_attr_32, L1_gnn_W1, L1_gnn_b1, L1_gnn_W2, L1_gnn_b2)
    return x

_drawn_inputs = setup_inputs


def setup_inputs(seed=0):
    import zlib

    import numpy as np

    out = dict(_drawn_inputs(seed))
    spreads = {'L0_gnn_b': (0.0, 0.1), 'L1_gnn_b2': (0.0, 0.1)}
    factors = {'L1_gnn_b1': 4.336}
    for name, (base, spread) in spreads.items():
        noise = np.random.default_rng([zlib.crc32(name.encode()), seed]).standard_normal(out[name].shape)
        drawn = base * np.exp(spread * noise) if base else spread * noise
        out[name] = jnp.asarray(drawn.astype(out[name].dtype))
    for name, factor in factors.items():
        out[name] = (out[name] * factor).astype(out[name].dtype)
    return out
```

```python
import concourse.bass as bass
from concourse import mybir
from contextlib import ExitStack

N, D, E = 100000, 48, 25000
DE, HID = 32, 128
P = 128
GT = 4
GE = GT * P
NG = -(-E // GE)
SLOTS = 3
ROWS = -(-N // P)
NPAD = ROWS * P
SPARE = GE
TABLE = NPAD + SPARE
CHUNK = 34
NC = ROWS // CHUNK
INIT = 131
EPS = 1e-5


def gnn_kernel(nc, x, ids, dst_rows, ew, ea, w, b, w1, b1, w2, b2, out):
    f32, i32 = mybir.dt.float32, mybir.dt.int32
    ALU, ACT, AX = mybir.AluOpType, mybir.ActivationFunctionType, mybir.AxisListType
    assert ROWS % CHUNK == 0 and (TABLE // P) % INIT == 0

    agg = nc.dram_tensor("agg", (TABLE, D), f32, kind="Internal").ap()
    x1 = nc.dram_tensor("x1", (NPAD, D), f32, kind="Internal").ap()

    x_v = x.rearrange("(p r) d -> p (r d)", p=P)
    agg_v = agg[0:NPAD, :].rearrange("(p r) d -> p (r d)", p=P)
    agg_all = agg.rearrange("(p r) d -> p (r d)", p=P)
    x1_v = x1.rearrange("(p r) d -> p (r d)", p=P)
    out_v = out[0:NPAD, :].rearrange("(p r) d -> p (r d)", p=P)
    out_spare = out[NPAD:TABLE, :].rearrange("(p r) d -> p (r d)", p=P)

    with ExitStack() as ctx:
        def sb(name, shape, dt=f32):
            return ctx.enter_context(nc.sbuf_tensor(name, shape, dt))

        def sem(name):
            return ctx.enter_context(nc.semaphore(name))

        def slot_sems(name):
            return [sem(f"{name}{s}") for s in range(SLOTS)]

        ident = sb("ident", [P, P])
        earlier = sb("earlier", [P, GE])
        spare_i = sb("spare_i", [P, GT], i32)
        spare = sb("spare", [P, GT])
        w_sb = sb("w_sb", [D + 1, D + 1])
        w1_sb = sb("w1_sb", [P, HID])
        w2_sb = sb("w2_sb", [HID, D])
        b1_sb = sb("b1_sb", [1, HID])
        ones = sb("ones", [1, P])
        b_sb = sb("b_sb", [P, D])
        b2_sb = sb("b2_sb", [P, D])
        eps = sb("eps", [P, 1])
        row_all = sb("row_all", [P, NG * GT], i32)
        count_all = sb("count_all", [P, NG * GT])
        idx = sb("idx", [P, SLOTS, 2 * GT], i32)
        row = sb("row", [P, SLOTS, GT], i32)
        weight = sb("weight", [P, SLOTS, GT])
        dst_row = sb("dst_row", [P, SLOTS, GE], i32)
        dst_col = sb("dst_col", [P, SLOTS, GT])
        raw = sb("raw", [P, SLOTS, GT, 2, D])
        cat = sb("cat", [P, SLOTS, GT, 2 * D + DE])
        same = sb("same", [P, SLOTS, GT, GE])
        wh = sb("wh", [P, SLOTS, GT, D + 1])
        xc = sb("xc", [P, SLOTS, 2 * GT, D])
        sq = sb("sq", [P, SLOTS, 2 * GT, D])
        var = sb("var", [P, SLOTS, 2 * GT])
        std = sb("std", [P, SLOTS, 2 * GT])
        sumT = sb("sumT", [P, SLOTS, GE])
        tot = sb("tot", [P, SLOTS, GT, D])
        scratch = sb("scratch", [P, GT, GE])
        n_before = sb("n_before", [P, GT])
        offset = sb("offset", [P, GT])
        lead = sb("lead", [P, GT])
        mean = sb("mean", [P, 2 * GT])
        rstd = sb("rstd", [P, 2 * GT])
        scale = sb("scale", [P, GT])
        bias2 = sb("bias2", [P, SLOTS, GT, D])
        catT = sb("catT", [P, GE])
        hid = sb("hid", [P, GT, HID])
        xbuf = sb("xbuf", [P, SLOTS, CHUNK * D])
        abuf = sb("abuf", [P, SLOTS, CHUNK * D])
        init = sb("init", [P, INIT, D])
        zero = sb("zero", [P, SPARE // P * D])

        def bank(name):
            return ctx.enter_context(nc.psum_tensor(name, [P, GE], f32))

        ps_sum = [bank(f"ps_sum{s}") for s in range(SLOTS)]
        ps_out = [bank(f"ps_out{s}") for s in range(SLOTS)]
        ps_catT = bank("ps_catT")
        ps_hid = bank("ps_hid")

        masks, masks_ready, spare_ready = sem("masks"), sem("masks_ready"), sem("spare_ready")
        consts_loaded, w_loaded, bias_loaded = sem("consts_loaded"), sem("w_loaded"), sem("bias_loaded")
        consts_set, init_ready, init_stored = sem("consts_set"), sem("init_ready"), sem("init_stored")
        zero_ready, spare_stored = sem("zero_ready"), sem("spare_stored")
        vector_step = sem("vector_step")

        pool_turns = sem("pool_turns")

        class Layer:
            def __init__(self, n):
                self.loaded = slot_sems(f"loaded{n}_")
                self.gathered = slot_sems(f"gathered{n}_")
                self.added = sem(f"added{n}")
                self.centred = sem(f"centred{n}")
                self.squared = sem(f"squared{n}")
                self.var_ready = sem(f"var_ready{n}")
                self.std_ready = sem(f"std_ready{n}")
                self.row_ready = sem(f"row_ready{n}")
                self.h_ready = sem(f"h_ready{n}")
                self.summed = sem(f"summed{n}")
                self.sumT_ready = sem(f"sumT_ready{n}")
                self.product = sem(f"product{n}")
                self.tot_ready = sem(f"tot_ready{n}")

        one, two = Layer(1), Layer(2)
        transposed, catT_ready = sem("transposed"), sem("catT_ready")
        hidden, hid_ready = sem("hidden"), sem("hid_ready")
        chunk_loaded, chunk_stored = slot_sems("chunk_loaded"), slot_sems("chunk_stored")
        chunk_ready = sem("chunk_ready")

        def wait(eng, s, value):
            if not isinstance(value, int) or value > 0:
                eng.wait_ge(s, value)

        def steps(eng, start, end, body):
            first = start if start and start % SLOTS == 0 else min(end, (start // SLOTS + 1) * SLOTS)
            turns = (end - first) // SLOTS
            for k in range(start, first):
                body(k, k % SLOTS, k // SLOTS)
            with eng.Fori(first // SLOTS, first // SLOTS + turns) as i:
                for s in range(SLOTS):
                    body(i * SLOTS + s, s, i)
            for k in range(first + turns * SLOTS, end):
                body(k, k % SLOTS, k // SLOTS)

        def last_store(eng):
            for s in range(SLOTS):
                eng.wait_ge(chunk_stored[s], 32 * len(range(s, NC, SLOTS)))

        block = ctx.enter_context(nc.Block())

        @block.sync
        def _(sp):
            sp.dma_start(b_sb[:, :], b.partition_broadcast(P)).then_inc(bias_loaded, 16)

            def load1(g, s, n):
                wait(sp, one.h_ready, g - SLOTS + 1)
                sp.dma_start(idx[:, s, :], ids[:, bass.ts(g, 2 * GT)]).then_inc(one.loaded[s], 16)
                sp.dma_start(dst_row[:, s, :], dst_rows[bass.ts(g, GE)].partition_broadcast(P)).then_inc(one.loaded[s], 16)
                sp.dma_start(weight[:, s, :], ew[:, bass.ts(g, GT)]).then_inc(one.loaded[s], 16)

            for g in range(SLOTS):
                load1(g, g, 0)
            sp.dma_start(b2_sb[:, :], b2.partition_broadcast(P)).then_inc(consts_loaded, 16)
            sp.dma_start(w1_sb[:, :], w1).then_inc(consts_loaded, 16)
            sp.dma_start(w2_sb[:, :], w2).then_inc(consts_loaded, 16)
            sp.dma_start(b1_sb[:, :], b1.rearrange("(a n) -> a n", a=1)).then_inc(consts_loaded, 16)
            sp.wait_ge(masks_ready, 1)
            sp.dma_start(w_sb[0:D, 0:D], w).then_inc(w_loaded, 16)
            sp.wait_ge(init_ready, 1)
            for c in range(TABLE // P // INIT):
                sp.dma_start(agg_all[:, c * INIT * D:(c + 1) * INIT * D], init[:, :, :].rearrange("p r d -> p (r d)"))\
                    .then_inc(init_stored, 16)
            steps(sp, SLOTS, NG, load1)

            def load_chunk(c, s, n):
                wait(sp, chunk_stored[s], n * 32)
                sp.dma_start(xbuf[:, s, :], x_v[:, bass.ts(c, CHUNK * D)]).then_inc(chunk_loaded[s], 16)
                sp.dma_start(abuf[:, s, :], agg_v[:, bass.ts(c, CHUNK * D)]).then_inc(chunk_loaded[s], 16)

            sp.wait_ge(one.added, 16 * GT * NG)
            steps(sp, 0, NC, load_chunk)

            def load2(g, s, n):
                wait(sp, two.h_ready, g - SLOTS + 1)
                wait(sp, transposed, g - SLOTS + 1)
                sp.dma_start(idx[:, s, :], ids[:, bass.ts(g, 2 * GT)]).then_inc(two.loaded[s], 16)
                sp.dma_start(dst_row[:, s, :], dst_rows[bass.ts(g, GE)].partition_broadcast(P)).then_inc(two.loaded[s], 16)
                sp.dma_start(cat[:, s, :, 2 * D:], ea[:, bass.ts(g, GT), :]).then_inc(two.loaded[s], 16)

            steps(sp, 0, NG, load2)
            sp.wait_ge(two.added, 16 * GT * NG)
            last_store(sp)
            sp.wait_ge(spare_stored, 16)

        @block.gpsimd
        def _(pool):
            nc.gpsimd.memset(ident[:, :], 0.0).then_inc(masks, 1)
            nc.gpsimd.memset(earlier[:, :], 1.0).then_inc(masks, 1)
            pool.wait_ge(masks, 2)
            nc.gpsimd.affine_select(out=ident[:, :], in_=ident[:, :], compare_op=ALU.not_equal, fill=1.0,
                                    base=0, pattern=[[-1, P]], channel_multiplier=1).then_inc(masks, 1)
            nc.gpsimd.affine_select(out=earlier[:, :], in_=earlier[:, :], compare_op=ALU.is_gt, fill=0.0,
                                    base=GE - P, pattern=[[-1, GE]], channel_multiplier=1).then_inc(masks, 1)
            pool.wait_ge(masks, 4)
            nc.gpsimd.tensor_copy(w_sb[:, :], ident[0:D + 1, 0:D + 1]).then_inc(masks_ready, 1)
            nc.gpsimd.iota(spare_i[:, :], pattern=[[P, GT]], base=NPAD, channel_multiplier=1).then_inc(spare_ready, 1)

            def gather(table, to, s, column, done):
                pool.indirect_dma_start(to, None, table, bass.IndirectOffsetOnAxis(ap=idx[:, s, column:column + 1], axis=0),
                                        bounds_check=NPAD - 1, oob_is_err=False).then_inc(done, 16)

            def gather1(g, s, n):
                pool.wait_ge(one.loaded[s], 48 * (n + 1))
                pool.sem_inc(pool_turns, 1)
                for t in range(GT):
                    gather(x, raw[:, s, t, 1, :], s, t, one.gathered[s])

            def gather2(g, s, n):
                pool.wait_ge(two.loaded[s], 48 * (n + 1))
                pool.sem_inc(pool_turns, 1)
                for t in range(GT):
                    gather(x1, raw[:, s, t, 0, :], s, GT + t, two.gathered[s])
                    gather(x1, raw[:, s, t, 1, :], s, t, two.gathered[s])

            def add(table, layer, g, s):
                pool.wait_ge(layer.row_ready, g + 1)
                pool.wait_ge(layer.tot_ready, g + 1)
                wait(pool, layer.added, g * (16 * GT))
                pool.sem_inc(pool_turns, 1)
                for t in range(GT):
                    pool.indirect_dma_start(table, bass.IndirectOffsetOnAxis(ap=row[:, s, t:t + 1], axis=0),
                                            tot[:, s, t, :], None, compute_op=ALU.add).then_inc(layer.added, 16)

            def run_layer(table, layer, gather_group):
                ahead = SLOTS - 1

                def step(k, s, n):
                    gather_group(k, s, n)
                    add(table, layer, k - ahead, (s - ahead) % SLOTS)

                steps(pool, ahead, NG, step)
                for g in range(NG - ahead, NG):
                    add(table, layer, g, g % SLOTS)

            for g in range(SLOTS - 1):
                gather1(g, g, 0)
            pool.wait_ge(init_stored, 16 * (TABLE // P // INIT))
            run_layer(agg, one, gather1)
            last_store(pool)
            pool.wait_ge(spare_stored, 16)
            for g in range(SLOTS - 1):
                gather2(g, g, 0)
            run_layer(out, two, gather2)

        @block.vector
        def _(dve):
            nc.vector.memset(ones[:, :], 1.0).then_inc(consts_set, 1)
            nc.vector.memset(eps[:, :], EPS).then_inc(consts_set, 1)
            nc.vector.memset(wh[:, :, :, D:D + 1], 1.0).then_inc(consts_set, 1)
            nc.vector.memset(zero[:, :], 0.0).then_inc(zero_ready, 1)
            dve.wait_ge(bias_loaded, 16)
            nc.vector.tensor_copy(init[:, :, :], b_sb[:, :].unsqueeze(1).broadcast_to([P, INIT, D])).then_inc(init_ready, 1)
            dve.wait_ge(spare_ready, 1)
            nc.vector.tensor_copy(spare[:, :], spare_i[:, :]).then_inc(consts_set, 1)
            dve.wait_ge(consts_set, 4)
            dve.wait_ge(masks, 4)

            def over_features(a):
                return a.unsqueeze(2).broadcast_to([P, a.shape[1], D])

            def chain(base):
                count = [0]

                def link(instruction):
                    instruction.then_inc(vector_step, 1)
                    count[0] += 1
                    dve.wait_ge(vector_step, base + count[0])
                return link, count

            def compare(s):
                for t in range(GT):
                    last = nc.vector.tensor_scalar(same[:, s, t, :], dst_row[:, s, :], dst_col[:, s, t:t + 1], None, ALU.is_equal)
                return last

            def centre(layer, s, rows, link):
                count = rows.shape[1]
                link(nc.vector.tensor_reduce(mean[:, 0:count], rows, AX.X, ALU.add))
                link(nc.vector.tensor_scalar(mean[:, 0:count], mean[:, 0:count], -1.0 / D, None, ALU.mult))
                nc.vector.tensor_tensor(xc[:, s, 0:count, :], rows, over_features(mean[:, 0:count]), ALU.add)\
                    .then_inc(layer.centred, 1)

            LINKS1 = 8

            def group1(g, s, n):
                link, links = chain(g * LINKS1)
                dve.wait_ge(one.loaded[s], 48 * (n + 1))
                link(nc.vector.tensor_copy(dst_col[:, s, :], idx[:, s, GT:2 * GT]))
                dve.wait_ge(one.gathered[s], 16 * GT * (n + 1))
                centre(one, s, raw[:, s, :, 1, :], link)
                wait(dve, one.summed, g - SLOTS + 1)
                compare(s)
                for t in range(GT):
                    last = nc.vector.scalar_tensor_tensor(
                        out=scratch[:, t, 0:(t + 1) * P], in0=dst_row[:, s, 0:(t + 1) * P], scalar=dst_col[:, s, t:t + 1],
                        in1=earlier[:, GE - (t + 1) * P:GE], op0=ALU.is_equal, op1=ALU.mult, accum_out=n_before[:, t:t + 1])
                dve.wait_ge(one.squared, g + 1)
                nc.vector.tensor_reduce(var[:, s, 0:GT], sq[:, s, 0:GT, :], AX.X, ALU.add).then_inc(one.var_ready, 1)
                link(last)
                link(nc.vector.tensor_tensor(offset[:, :], dst_col[:, s, :], spare[:, :], ALU.subtract))
                link(nc.vector.scalar_tensor_tensor(out=lead[:, :], in0=n_before[:, :], scalar=0.0, in1=offset[:, :],
                                                    op0=ALU.is_equal, op1=ALU.mult))
                wait(dve, one.added, (g - SLOTS + 1) * (16 * GT))
                nc.vector.tensor_tensor(row_all[:, bass.ts(g, GT)], lead[:, :], spare[:, :], ALU.add)
                nc.vector.tensor_tensor(row[:, s, :], lead[:, :], spare[:, :], ALU.add).then_inc(one.row_ready, 1)
                dve.wait_ge(one.std_ready, g + 1)
                link(nc.vector.reciprocal(rstd[:, 0:GT], std[:, s, 0:GT]))
                link(nc.vector.tensor_tensor(scale[:, :], rstd[:, 0:GT], weight[:, s, :], ALU.mult))
                nc.vector.scalar_tensor_tensor(out=wh[:, s, :, 0:D], in0=xc[:, s, 0:GT, :], scalar=0.0,
                                               in1=over_features(scale[:, :]), op0=ALU.max, op1=ALU.mult).then_inc(one.h_ready, 1)
                assert links[0] == LINKS1, links

            steps(dve, 0, NG, group1)

            def chunk(c, s, n):
                dve.wait_ge(chunk_loaded[s], 32 * (n + 1))
                nc.vector.scalar_tensor_tensor(out=xbuf[:, s, :], in0=abuf[:, s, :], scalar=0.0, in1=xbuf[:, s, :],
                                               op0=ALU.max, op1=ALU.add).then_inc(chunk_ready, 1)

            steps(dve, 0, NC, chunk)
            dve.wait_ge(consts_loaded, 64)

            def total2(g, s, link):
                link(nc.vector.tensor_tensor(bias2[:, s, :, :], b2_sb[:, :].unsqueeze(1).broadcast_to([P, GT, D]),
                                             over_features(count_all[:, bass.ts(g, GT)]), ALU.mult))
                dve.wait_ge(two.product, g + 1)
                nc.vector.tensor_tensor(tot[:, s, :, :], ps_out[s][:, 0:GT * D].rearrange("p (t d) -> p t d", t=GT),
                                        bias2[:, s, :, :], ALU.add).then_inc(two.tot_ready, 1)

            LINKS2 = 5

            def group2(g, s, n):
                link, links = chain(g * LINKS2 + NG * LINKS1)
                dve.wait_ge(two.loaded[s], 48 * (n + 1))
                link(nc.vector.tensor_copy(dst_col[:, s, :], idx[:, s, GT:2 * GT]))
                dve.wait_ge(two.gathered[s], 32 * GT * (n + 1))
                centre(two, s, raw[:, s, :, :, :].rearrange("p t k d -> p (t k) d"), link)
                wait(dve, two.summed, g - SLOTS + 1)
                compare(s)
                dve.wait_ge(two.squared, g + 1)
                nc.vector.tensor_reduce(var[:, s, :], sq[:, s, :, :], AX.X, ALU.add).then_inc(two.var_ready, 1)
                wait(dve, two.added, (g - SLOTS + 1) * (16 * GT))
                nc.vector.tensor_copy(row[:, s, :], row_all[:, bass.ts(g, GT)]).then_inc(two.row_ready, 1)
                dve.wait_ge(two.std_ready, g + 1)
                link(nc.vector.reciprocal(rstd[:, :], std[:, s, :]))
                for k in range(2):
                    scales = rstd[:, :].rearrange("p (t k) -> p k t", k=2)[:, k, :]
                    last = nc.vector.scalar_tensor_tensor(
                        out=cat[:, s, :, k * D:(k + 1) * D], in0=xc[:, s, :, :].rearrange("p (t k) d -> p k t d", k=2)[:, k, :, :],
                        scalar=0.0, in1=over_features(scales), op0=ALU.max, op1=ALU.mult)
                last.then_inc(two.h_ready, 1)
                if not isinstance(g, int) or g > 0:
                    total2(g - 1, (s - 1) % SLOTS, link)
                else:
                    link(nc.vector.memset(scratch[:, 0, 0:1], 0.0))
                assert links[0] == LINKS2, links

            steps(dve, 0, NG, group2)
            total2(NG - 1, (NG - 1) % SLOTS, chain(NG * (LINKS1 + LINKS2))[0])

        @block.scalar
        def _(act):
            act.wait_ge(zero_ready, 1)
            act.dma_start(out_spare, zero[:, :]).then_inc(spare_stored, 16)
            act.wait_ge(consts_set, 4)

            def square(layer, g, s, count):
                act.wait_ge(layer.centred, g + 1)
                nc.scalar.activation(sq[:, s, 0:count, :], xc[:, s, 0:count, :], ACT.Square).then_inc(layer.squared, 1)

            def root(layer, g, s, count):
                act.wait_ge(layer.var_ready, g + 1)
                nc.scalar.activation(std[:, s, 0:count], var[:, s, 0:count], ACT.Sqrt, scale=1.0 / D, bias=eps[:, :])\
                    .then_inc(layer.std_ready, 1)

            def sums(layer, g, s, height):
                act.wait_ge(layer.summed, g + 1)
                wait(act, layer.product, g - SLOTS + 1)
                nc.scalar.activation(sumT[0:height, s, :], ps_sum[s][0:height, :], ACT.Copy).then_inc(layer.sumT_ready, 1)

            def total1(g, s):
                act.wait_ge(one.product, g + 1)
                wait(act, one.added, (g - SLOTS + 1) * (16 * GT))
                product = ps_out[s][:, 0:GT * (D + 1)].rearrange("p (t d) -> p t d", t=GT)
                nc.scalar.activation(count_all[:, bass.ts(g, GT)], product[:, :, D], ACT.Copy)
                nc.scalar.activation(tot[:, s, :, :], product[:, :, 0:D], ACT.Copy).then_inc(one.tot_ready, 1)

            def group1(g, s, n):
                square(one, g, s, GT)
                if not isinstance(g, int) or g > 0:
                    sums(one, g - 1, (s - 1) % SLOTS, D + 1)
                root(one, g, s, GT)
                if not isinstance(g, int) or g > 0:
                    total1(g - 1, (s - 1) % SLOTS)

            steps(act, 0, NG, group1)
            sums(one, NG - 1, (NG - 1) % SLOTS, D + 1)
            total1(NG - 1, (NG - 1) % SLOTS)

            def store_chunk(c, s, n):
                act.wait_ge(chunk_ready, c + 1)
                act.dma_start(x1_v[:, bass.ts(c, CHUNK * D)], xbuf[:, s, :]).then_inc(chunk_stored[s], 16)
                act.dma_start(out_v[:, bass.ts(c, CHUNK * D)], xbuf[:, s, :]).then_inc(chunk_stored[s], 16)

            steps(act, 0, NC, store_chunk)

            def group2(g, s, n):
                square(two, g, s, 2 * GT)
                if not isinstance(g, int) or g > 0:
                    sums(two, g - 1, (s - 1) % SLOTS, P)
                root(two, g, s, 2 * GT)
                act.wait_ge(transposed, g + 1)
                nc.scalar.activation(catT[:, :], ps_catT[:, :], ACT.Copy).then_inc(catT_ready, 1)
                act.wait_ge(hidden, g + 1)
                nc.scalar.activation(hid[:, :, :].rearrange("p t d -> p (t d)"), ps_hid[:, :], ACT.Relu).then_inc(hid_ready, 1)

            steps(act, 0, NG, group2)
            sums(two, NG - 1, (NG - 1) % SLOTS, P)

        @block.tensor
        def _(pe):
            pe.wait_ge(masks, 4)
            pe.wait_ge(consts_set, 4)
            pe.wait_ge(consts_loaded, 64)
            pe.wait_ge(w_loaded, 16)

            def tile(t, width=P):
                return slice(t * width, (t + 1) * width)

            def node_sums(layer, g, s, left, height):
                for t in range(GT):
                    last = nc.tensor.matmul(ps_sum[s][0:height, :], left[:, t, :], same[:, s, t, :],
                                            start=t == 0, stop=t == GT - 1)
                last.then_inc(layer.summed, 1)

            def product(layer, g, s, right, height, width):
                pe.wait_ge(layer.sumT_ready, g + 1)
                wait(pe, layer.tot_ready, g - SLOTS + 1)
                for t in range(GT):
                    last = nc.tensor.matmul(ps_out[s][:, tile(t, width)], sumT[0:height, s, tile(t)], right,
                                            start=True, stop=True)
                last.then_inc(layer.product, 1)

            def group1(g, s, n):
                if not isinstance(g, int) or g > 0:
                    product(one, g - 1, (s - 1) % SLOTS, w_sb[:, :], D + 1, D + 1)
                pe.wait_ge(one.h_ready, g + 1)
                node_sums(one, g, s, wh[:, s, :, :], D + 1)

            steps(pe, 0, NG, group1)
            product(one, NG - 1, (NG - 1) % SLOTS, w_sb[:, :], D + 1, D + 1)

            def group2(g, s, n):
                if not isinstance(g, int) or g > 0:
                    product(two, g - 1, (s - 1) % SLOTS, w2_sb[:, :], HID, D)
                pe.wait_ge(two.h_ready, g + 1)
                for t in range(GT):
                    last = nc.tensor.transpose(ps_catT[:, tile(t)], cat[:, s, t, :], ident[:, :])
                last.then_inc(transposed, 1)
                pe.wait_ge(catT_ready, g + 1)
                for t in range(GT):
                    nc.tensor.matmul(ps_hid[:, tile(t)], catT[:, tile(t)], w1_sb[:, :], start=True, stop=False)
                    last = nc.tensor.matmul(ps_hid[:, tile(t)], ones[:, :], b1_sb[:, :], start=False, stop=True)
                last.then_inc(hidden, 1)
                pe.wait_ge(hid_ready, g + 1)
                node_sums(two, g, s, hid, P)

            steps(pe, 0, NG, group2)
            product(two, NG - 1, (NG - 1) % SLOTS, w2_sb[:, :], HID, D)


def kernel(x, src, dst, edge_attr_32, edge_weight, L0_gnn_w, L0_gnn_b, L1_gnn_W1, L1_gnn_b1, L1_gnn_W2, L1_gnn_b2):
    import numpy as np
    import concourse.bacc as bacc
    from concourse.bass_utils import run_bass_kernel_spmd

    pad = NG * GE - E

    def tiles(a, fill):
        a = np.asarray(a)
        a = np.concatenate([a, np.full((pad,) + a.shape[1:], fill, a.dtype)])
        return np.ascontiguousarray(a.reshape((NG * GT, P) + a.shape[1:]).swapaxes(0, 1))

    src_t, dst_t = (tiles(a, fill).reshape(P, NG, GT) for a, fill in ((src, 0), (dst, N)))
    arrays = {
        "x": np.concatenate([np.asarray(x), np.zeros((NPAD - N, D), np.float32)]),
        "ids": np.ascontiguousarray(np.stack([src_t, dst_t], 2)).reshape(P, NG * 2 * GT),
        "dst_rows": np.concatenate([np.asarray(dst), np.full(pad, N, np.asarray(dst).dtype)]),
        "ew": tiles(edge_weight, 0),
        "ea": tiles(edge_attr_32, 0),
        "w": np.asarray(L0_gnn_w), "b": np.asarray(L0_gnn_b),
        "w1": np.asarray(L1_gnn_W1), "b1": np.asarray(L1_gnn_b1),
        "w2": np.asarray(L1_gnn_W2), "b2": np.asarray(L1_gnn_b2),
    }
    nc = bacc.Bacc("TRN2", target_bir_lowering=False, num_devices=1)
    args = {k: nc.dram_tensor(f"in_{k}", a.shape, mybir.dt.from_np(a.dtype), kind="ExternalInput").ap()
            for k, a in arrays.items()}
    out = nc.dram_tensor("out_rows", (TABLE, D), mybir.dt.float32, kind="ExternalOutput").ap()
    gnn_kernel(nc, **args, out=out)
    r = run_bass_kernel_spmd(nc, [{f"in_{k}": a for k, a in arrays.items()}], core_ids=[0])
    return r.results[0]["out_rows"][:N]
```

```python
import concourse.bass as bass
from concourse import mybir
from contextlib import ExitStack

N, D, E = 100000, 48, 25000
DE, HID = 32, 128
P = 128
GT = 4
GE = GT * P
NG = -(-E // GE)
SLOTS = 4
AHEAD1, AHEAD2 = 36, 36
ROWS = -(-N // P)
NPAD = ROWS * P
SPARE = GE
TABLE = NPAD + SPARE
CHUNK = 23
NC = ROWS // CHUNK
BESIDE1, BESIDE2 = 2, 3
EPS = 1e-5


def gnn_kernel(nc, x, ids, dst_rows, ew, ea, w, b, w1, b1, w2, b2, out):
    f32, i32 = mybir.dt.float32, mybir.dt.int32
    ALU, ACT, AX = mybir.AluOpType, mybir.ActivationFunctionType, mybir.AxisListType
    assert ROWS % CHUNK == 0 and NC <= AHEAD1 < NG - 2 and NC <= AHEAD2 < NG - 2 and AHEAD1 % SLOTS == AHEAD2 % SLOTS == 0

    table = nc.dram_tensor("table", (TABLE, 2 * D), f32, kind="Internal").ap()
    table_parts = table.rearrange("n (k d) -> (n k) d", k=2)

    x_v = x.rearrange("(p r) d -> p (r d)", p=P)
    table_v = table[0:NPAD, :].rearrange("(p r) d -> p (r d)", p=P)
    table_spare = table[NPAD:TABLE, :].rearrange("(p r) d -> p (r d)", p=P)
    out_v = out[0:NPAD, :].rearrange("(p r) d -> p (r d)", p=P)
    out_spare = out[NPAD:TABLE, :].rearrange("(p r) d -> p (r d)", p=P)

    with ExitStack() as ctx:
        def sb(name, shape, dt=f32):
            return ctx.enter_context(nc.sbuf_tensor(name, shape, dt))

        def sem(name):
            return ctx.enter_context(nc.semaphore(name))

        def slot_sems(name):
            return [sem(f"{name}{s}") for s in range(SLOTS)]

        ident = sb("ident", [P, P])
        earlier = sb("earlier", [P, GE])
        spare_i = sb("spare_i", [P, GT], i32)
        spare = sb("spare", [P, GT])
        w_sb = sb("w_sb", [D + 1, D + 1])
        w1_sb = sb("w1_sb", [P, HID])
        w2_sb = sb("w2_sb", [HID, D])
        b1_sb = sb("b1_sb", [1, HID])
        ones = sb("ones", [1, P])
        b_sb = sb("b_sb", [P, D])
        b2_sb = sb("b2_sb", [P, D])
        eps = sb("eps", [P, 1])
        sum_row_all = sb("sum_row_all", [P, NG * GT], i32)
        row_all = sb("row_all", [P, NG * GT], i32)
        tot_all = sb("tot_all", [P, NG * GT * D])
        count_all = sb("count_all", [P, NG * GT])
        idx = sb("idx", [P, SLOTS, 2 * GT], i32)
        weight = sb("weight", [P, SLOTS, GT])
        dst_row = sb("dst_row", [P, SLOTS, GE], i32)
        dst_col = sb("dst_col", [P, SLOTS, GT])
        raw1 = sb("raw1", [P, SLOTS, GT, D])
        raw2 = sb("raw2", [P, SLOTS, GT, 2, 2 * D])
        x1 = sb("x1", [P, SLOTS, 2 * GT, D])
        cat = sb("cat", [P, SLOTS, GT, 2 * D + DE])
        same = sb("same", [P, 2, GT, GE])
        wh = sb("wh", [P, SLOTS, GT, D + 1])
        xc = sb("xc", [P, SLOTS, 2 * GT, D])
        sq = sb("sq", [P, SLOTS, 2 * GT, D])
        var = sb("var", [P, SLOTS, 2 * GT])
        std = sb("std", [P, SLOTS, 2 * GT])
        sumT = sb("sumT", [P, 2, GE])
        row = sb("row", [P, SLOTS * max(BESIDE1, BESIDE2), GT], i32)
        tot = sb("tot", [P, SLOTS * max(BESIDE1, BESIDE2), GT * D])
        scratch = sb("scratch", [P, GT, GE], mybir.dt.bfloat16)
        n_before = sb("n_before", [P, GT])
        offset = sb("offset", [P, GT])
        lead = sb("lead", [P, GT])
        row_f = sb("row_f", [P, GT])
        total = sb("total", [P, 2 * GT])
        rstd = sb("rstd", [P, 2 * GT])
        scale = sb("scale", [P, GT])
        bias2 = sb("bias2", [P, SLOTS, GT, D])
        catT = sb("catT", [P, GE])
        hid = sb("hid", [P, GT, HID])
        node_rows = sb("node_rows", [P, SLOTS, CHUNK, 2, D])
        x_rows = sb("x_rows", [P, SLOTS, CHUNK, D])
        zero = sb("zero", [P, SPARE // P * 2 * D])

        def bank(name):
            return ctx.enter_context(nc.psum_tensor(name, [P, GE], f32))

        ps_sum = [bank(f"ps_sum{s}") for s in range(2)]
        ps_out = [bank(f"ps_out{s}") for s in range(2)]
        ps_catT = bank("ps_catT")
        ps_hid = bank("ps_hid")

        masks, masks_ready, spare_ready = sem("masks"), sem("masks_ready"), sem("spare_ready")
        consts_loaded, w_loaded, bias_loaded = sem("consts_loaded"), sem("w_loaded"), sem("bias_loaded")
        consts_set, bias_filled = sem("consts_set"), sem("bias_filled")
        zero_ready, spare_stored = sem("zero_ready"), sem("spare_stored")
        vector_step = sem("vector_step")

        pool_turns = sem("pool_turns")

        class Layer:
            def __init__(self, n):
                self.loaded = slot_sems(f"loaded{n}_")
                self.gathered = slot_sems(f"gathered{n}_")
                self.added = sem(f"added{n}")
                self.centred = sem(f"centred{n}")
                self.squared = sem(f"squared{n}")
                self.var_ready = sem(f"var_ready{n}")
                self.std_ready = sem(f"std_ready{n}")
                self.row_ready = sem(f"row_ready{n}")
                self.h_ready = sem(f"h_ready{n}")
                self.summed = sem(f"summed{n}")
                self.sumT_ready = sem(f"sumT_ready{n}")
                self.product = sem(f"product{n}")
                self.tot_ready = sem(f"tot_ready{n}")
                self.staged = sem(f"staged{n}")

        one, two = Layer(1), Layer(2)
        transposed, catT_ready = sem("transposed"), sem("catT_ready")
        hidden, hid_ready = sem("hidden"), sem("hid_ready")
        x_loaded, table_stored = slot_sems("x_loaded"), slot_sems("table_stored")
        x_placed = sem("x_placed")
        rows_loaded, out_stored = slot_sems("rows_loaded"), slot_sems("out_stored")
        out_ready = sem("out_ready")

        def wait(eng, s, value):
            if not isinstance(value, int) or value > 0:
                eng.wait_ge(s, value)

        def steps(eng, start, end, body, turn=SLOTS):
            first = min(end, (start // turn + 1) * turn)
            turns = max(0, end - first) // turn
            for k in range(start, first):
                body(k, k % turn, k // turn)
            if turns:
                with eng.Fori(first // turn, first // turn + turns) as i:
                    for s in range(turn):
                        body(i * turn + s, s, i)
            for k in range(first + turns * turn, end):
                body(k, k % turn, k // turn)

        def phases(eng, body, *flags, cut=0):
            cuts = sorted({0, cut, NG, *(c for f in flags for c in f)})
            for a, z in zip(cuts, cuts[1:]):
                on = [f[0] <= a < f[1] for f in flags]
                steps(eng, a, z, lambda k, s, n: body(k, s, n, *on))

        def begun(g, back=1):
            return not isinstance(g, int) or g >= back

        block = ctx.enter_context(nc.Block())

        @block.sync
        def _(sp):
            sp.dma_start(b_sb[:, :], b.partition_broadcast(P)).then_inc(bias_loaded, 16)

            def load_x(c, s, n):
                wait(sp, x_placed, c - SLOTS + 1)
                sp.dma_start(x_rows[:, s, :, :].rearrange("p r d -> p (r d)"), x_v[:, bass.ts(c, CHUNK * D)])\
                    .then_inc(x_loaded[s], 16)

            def load1(g, s, n):
                wait(sp, one.h_ready, g - SLOTS + 1)
                sp.dma_start(idx[:, s, :], ids[:, bass.ts(g, 2 * GT)]).then_inc(one.loaded[s], 16)
                sp.dma_start(dst_row[:, s, :], dst_rows[bass.ts(g, GE)].partition_broadcast(P)).then_inc(one.loaded[s], 16)
                sp.dma_start(weight[:, s, :], ew[:, bass.ts(g, GT)]).then_inc(one.loaded[s], 16)

            def load_both(g, s, n, with_x=True):
                load1(g, s, n)
                if with_x:
                    load_x(g, s, n)

            for g in range(SLOTS):
                load_both(g, g, 0)
            sp.dma_start(b2_sb[:, :], b2.partition_broadcast(P)).then_inc(consts_loaded, 16)
            sp.dma_start(w1_sb[:, :], w1).then_inc(consts_loaded, 16)
            sp.dma_start(w2_sb[:, :], w2).then_inc(consts_loaded, 16)
            sp.dma_start(b1_sb[:, :], b1.rearrange("(a n) -> a n", a=1)).then_inc(consts_loaded, 16)
            sp.wait_ge(masks_ready, 1)
            sp.dma_start(w_sb[0:D, 0:D], w).then_inc(w_loaded, 16)
            steps(sp, SLOTS, NC, load_both)
            steps(sp, NC, NG, lambda g, s, n: load_both(g, s, n, False))

            def load2(g, s, n):
                wait(sp, two.h_ready, g - SLOTS + 1)
                wait(sp, transposed, g - SLOTS + 1)
                sp.dma_start(idx[:, s, :], ids[:, bass.ts(g, 2 * GT)]).then_inc(two.loaded[s], 16)
                sp.dma_start(dst_row[:, s, :], dst_rows[bass.ts(g, GE)].partition_broadcast(P)).then_inc(two.loaded[s], 16)
                sp.dma_start(cat[:, s, :, 2 * D:], ea[:, bass.ts(g, GT), :]).then_inc(two.loaded[s], 16)

            def load_rows(c, s, n):
                wait(sp, out_ready, c - SLOTS + 1)
                sp.dma_start(node_rows[:, s, :, :, :].rearrange("p r k d -> p (r k d)"),
                             table_v[:, bass.ts(c, CHUNK * 2 * D)]).then_inc(rows_loaded[s], 16)

            def load2_rows(g, s, n, with_rows):
                load2(g, s, n)
                if with_rows:
                    load_rows(g, s, n)

            sp.wait_ge(one.added, 16 * GT * NG)
            phases(sp, load2_rows, (0, NC))
            sp.wait_ge(two.added, 16 * GT * NG)
            for s in range(SLOTS):
                sp.wait_ge(out_stored[s], 16 * len(range(s, NC, SLOTS)))
            sp.wait_ge(spare_stored, 32)

        @block.gpsimd
        def _(pool):
            nc.gpsimd.memset(ident[:, :], 0.0).then_inc(masks, 1)
            nc.gpsimd.memset(earlier[:, :], 1.0).then_inc(masks, 1)
            pool.wait_ge(masks, 2)
            nc.gpsimd.affine_select(out=ident[:, :], in_=ident[:, :], compare_op=ALU.not_equal, fill=1.0,
                                    base=0, pattern=[[-1, P]], channel_multiplier=1).then_inc(masks, 1)
            nc.gpsimd.affine_select(out=earlier[:, :], in_=earlier[:, :], compare_op=ALU.is_gt, fill=0.0,
                                    base=GE - P, pattern=[[-1, GE]], channel_multiplier=1).then_inc(masks, 1)
            pool.wait_ge(masks, 4)
            nc.gpsimd.tensor_copy(w_sb[:, :], ident[0:D + 1, 0:D + 1]).then_inc(masks_ready, 1)
            nc.gpsimd.iota(spare_i[:, :], pattern=[[P, GT]], base=NPAD, channel_multiplier=1).then_inc(spare_ready, 1)

            def gather(source, to, s, column, done):
                pool.indirect_dma_start(to, None, source, bass.IndirectOffsetOnAxis(ap=idx[:, s, column:column + 1], axis=0),
                                        bounds_check=NPAD - 1, oob_is_err=False).then_inc(done, 16)

            def gather1(g, s, n, tiles):
                pool.wait_ge(one.loaded[s], 48 * (n + 1))
                pool.sem_inc(pool_turns, 1)
                for t in tiles:
                    gather(x, raw1[:, s, t, :], s, t, one.gathered[s])

            def gather2(g, s, n, tiles):
                pool.wait_ge(two.loaded[s], 48 * (n + 1))
                pool.sem_inc(pool_turns, 1)
                for t in tiles:
                    gather(table, raw2[:, s, t, 0, :], s, GT + t, two.gathered[s])
                    gather(table, raw2[:, s, t, 1, :], s, t, two.gathered[s])

            def add(to, layer, g, o):
                pool.wait_ge(layer.staged, g + 1)
                wait(pool, layer.added, g * (16 * GT))
                pool.sem_inc(pool_turns, 1)
                for t in range(GT):
                    pool.indirect_dma_start(to, bass.IndirectOffsetOnAxis(ap=row[:, o, t:t + 1], axis=0),
                                            tot[:, o, t * D:(t + 1) * D], None, compute_op=ALU.add).then_inc(layer.added, 16)

            def run_layer(to, layer, gather_group, ahead, beside, start_ready):
                steps(pool, 0, ahead, lambda g, s, n: gather_group(g, s, n, range(GT)))
                start_ready()

                def gather_and_add(k, s, n):
                    for q in range(beside):
                        gather_group(k, s, n, range(q * GT // beside, (q + 1) * GT // beside))
                        add(to, layer, k * beside + (q - beside * ahead), beside * s + q)

                steps(pool, ahead, NG, gather_and_add)
                steps(pool, beside * (NG - ahead), NG, lambda g, o, n: add(to, layer, g, o), turn=SLOTS * beside)

            def table_ready():
                for s in range(SLOTS):
                    pool.wait_ge(table_stored[s], 16 * len(range(s, NC, SLOTS)))
                pool.wait_ge(spare_stored, 32)

            def out_started():
                for s in range(SLOTS):
                    pool.wait_ge(out_stored[s], 16 * len(range(s, NC, SLOTS)))

            run_layer(table_parts, one, gather1, AHEAD1, BESIDE1, table_ready)
            pool.wait_ge(one.added, 16 * GT * NG)
            run_layer(out, two, gather2, AHEAD2, BESIDE2, out_started)

        @block.vector
        def _(dve):
            nc.vector.memset(ones[:, :], 1.0).then_inc(consts_set, 1)
            nc.vector.memset(eps[:, :], EPS).then_inc(consts_set, 1)
            nc.vector.memset(wh[:, :, :, D:D + 1], 1.0).then_inc(consts_set, 1)
            nc.vector.memset(zero[:, :], 0.0).then_inc(zero_ready, 1)
            dve.wait_ge(bias_loaded, 16)
            for s in range(SLOTS):
                nc.vector.tensor_copy(node_rows[:, s, :, 1, :], b_sb[:, :].unsqueeze(1).broadcast_to([P, CHUNK, D]))\
                    .then_inc(bias_filled, 1)
            dve.wait_ge(spare_ready, 1)
            nc.vector.tensor_copy(spare[:, :], spare_i[:, :]).then_inc(consts_set, 1)
            dve.wait_ge(consts_set, 4)
            dve.wait_ge(masks, 4)

            def over_features(a):
                return a.unsqueeze(2).broadcast_to([P, a.shape[1], D])

            def chain(base):
                count = [0]

                def link(instruction):
                    instruction.then_inc(vector_step, 1)
                    count[0] += 1
                    dve.wait_ge(vector_step, base + count[0])
                return link, count

            def compare(s):
                for t in range(GT):
                    last = nc.vector.tensor_scalar(same[:, s % 2, t, :], dst_row[:, s, :], dst_col[:, s, t:t + 1], None, ALU.is_equal)
                return last

            def centre(layer, s, rows, link):
                count = rows.shape[1]
                link(nc.vector.tensor_reduce(total[:, 0:count], rows, AX.X, ALU.add))
                nc.vector.scalar_tensor_tensor(out=xc[:, s, 0:count, :], in0=over_features(total[:, 0:count]), scalar=-1.0 / D,
                                               in1=rows, op0=ALU.mult, op1=ALU.add).then_inc(layer.centred, 1)

            LINKS1 = 8

            def group1(g, s, n):
                link, links = chain(g * LINKS1)
                dve.wait_ge(one.loaded[s], 48 * (n + 1))
                link(nc.vector.tensor_copy(dst_col[:, s, :], idx[:, s, GT:2 * GT]))
                dve.wait_ge(one.gathered[s], 16 * GT * (n + 1))
                centre(one, s, raw1[:, s, :, :], link)
                wait(dve, one.summed, g - 1)
                compare(s)
                for t in range(GT):
                    last = nc.vector.scalar_tensor_tensor(
                        out=scratch[:, t, 0:(t + 1) * P], in0=dst_row[:, s, 0:(t + 1) * P], scalar=dst_col[:, s, t:t + 1],
                        in1=earlier[:, GE - (t + 1) * P:GE], op0=ALU.is_equal, op1=ALU.mult, accum_out=n_before[:, t:t + 1])
                dve.wait_ge(one.squared, g + 1)
                nc.vector.tensor_reduce(var[:, s, 0:GT], sq[:, s, 0:GT, :], AX.X, ALU.add).then_inc(one.var_ready, 1)
                link(last)
                link(nc.vector.tensor_tensor(offset[:, :], dst_col[:, s, :], spare[:, :], ALU.subtract))
                link(nc.vector.scalar_tensor_tensor(out=lead[:, :], in0=n_before[:, :], scalar=0.0, in1=offset[:, :],
                                                    op0=ALU.is_equal, op1=ALU.mult))
                link(nc.vector.tensor_tensor(row_f[:, :], lead[:, :], spare[:, :], ALU.add))
                nc.vector.tensor_copy(row_all[:, bass.ts(g, GT)], row_f[:, :])
                nc.vector.tensor_scalar(sum_row_all[:, bass.ts(g, GT)], row_f[:, :], 2.0, 1.0, ALU.mult, ALU.add)\
                    .then_inc(one.row_ready, 1)
                dve.wait_ge(one.std_ready, g + 1)
                link(nc.vector.reciprocal(rstd[:, 0:GT], std[:, s, 0:GT]))
                link(nc.vector.tensor_tensor(scale[:, :], rstd[:, 0:GT], weight[:, s, :], ALU.mult))
                nc.vector.scalar_tensor_tensor(out=wh[:, s, :, 0:D], in0=xc[:, s, 0:GT, :], scalar=0.0,
                                               in1=over_features(scale[:, :]), op0=ALU.max, op1=ALU.mult).then_inc(one.h_ready, 1)
                assert links[0] == LINKS1, links

            steps(dve, 0, NG, group1)

            dve.wait_ge(consts_loaded, 64)

            def total2(g, s, link):
                link(nc.vector.tensor_tensor(bias2[:, s, :, :], b2_sb[:, :].unsqueeze(1).broadcast_to([P, GT, D]),
                                             over_features(count_all[:, bass.ts(g, GT)]), ALU.mult))
                dve.wait_ge(two.product, g + 1)
                nc.vector.tensor_tensor(tot_all[:, bass.ts(g, GT * D)], ps_out[s % 2][:, 0:GT * D],
                                        bias2[:, s, :, :].rearrange("p t d -> p (t d)"), ALU.add).then_inc(two.tot_ready, 1)

            LINKS2 = 5

            def group2(g, s, n):
                link, links = chain(g * LINKS2 + NG * LINKS1)
                dve.wait_ge(two.loaded[s], 48 * (n + 1))
                link(nc.vector.tensor_copy(dst_col[:, s, :], idx[:, s, GT:2 * GT]))
                dve.wait_ge(two.gathered[s], 32 * GT * (n + 1))
                parts = raw2[:, s, :, :, :].rearrange("p t k d -> p (t k) d")
                link(nc.vector.scalar_tensor_tensor(out=x1[:, s, :, :], in0=parts[:, :, D:2 * D], scalar=0.0,
                                                    in1=parts[:, :, 0:D], op0=ALU.max, op1=ALU.add))
                centre(two, s, x1[:, s, :, :], link)
                wait(dve, two.summed, g - 1)
                compare(s)
                dve.wait_ge(two.squared, g + 1)
                nc.vector.tensor_reduce(var[:, s, :], sq[:, s, :, :], AX.X, ALU.add).then_inc(two.var_ready, 1)
                if begun(g, 2):
                    total2(g - 2, (s - 2) % SLOTS, link)
                else:
                    link(nc.vector.memset(scratch[:, 0, 0:1], 0.0))
                dve.wait_ge(two.std_ready, g + 1)
                link(nc.vector.reciprocal(rstd[:, :], std[:, s, :]))
                for k in range(2):
                    scales = rstd[:, :].rearrange("p (t k) -> p k t", k=2)[:, k, :]
                    last = nc.vector.scalar_tensor_tensor(
                        out=cat[:, s, :, k * D:(k + 1) * D], in0=xc[:, s, :, :].rearrange("p (t k) d -> p k t d", k=2)[:, k, :, :],
                        scalar=0.0, in1=over_features(scales), op0=ALU.max, op1=ALU.mult)
                last.then_inc(two.h_ready, 1)
                assert links[0] == LINKS2, links

            def start_out(c, s, n):
                dve.wait_ge(rows_loaded[s], (n + 1) * 16)
                wait(dve, out_stored[s], n * 16)
                nc.vector.scalar_tensor_tensor(out=x_rows[:, s, :, :], in0=node_rows[:, s, :, 1, :], scalar=0.0,
                                               in1=node_rows[:, s, :, 0, :], op0=ALU.max, op1=ALU.add).then_inc(out_ready, 1)

            def group2_rows(g, s, n, with_rows):
                group2(g, s, n)
                if with_rows:
                    start_out(g, s, n)

            phases(dve, group2_rows, (0, NC))
            link, _ = chain(NG * (LINKS1 + LINKS2))
            for g in (NG - 2, NG - 1):
                total2(g, g % SLOTS, link)

        @block.scalar
        def _(act):
            act.wait_ge(zero_ready, 1)
            act.dma_start(out_spare, zero[:, 0:SPARE // P * D]).then_inc(spare_stored, 16)
            act.dma_start(table_spare, zero[:, :]).then_inc(spare_stored, 16)
            act.wait_ge(consts_set, 4)

            def square(layer, g, s, count):
                act.wait_ge(layer.centred, g + 1)
                nc.scalar.activation(sq[:, s, 0:count, :], xc[:, s, 0:count, :], ACT.Square).then_inc(layer.squared, 1)

            def root(layer, g, s, count):
                act.wait_ge(layer.var_ready, g + 1)
                nc.scalar.activation(std[:, s, 0:count], var[:, s, 0:count], ACT.Sqrt, scale=1.0 / D, bias=eps[:, :])\
                    .then_inc(layer.std_ready, 1)

            def sums(layer, g, s, height):
                act.wait_ge(layer.summed, g + 1)
                wait(act, layer.product, g - 1)
                nc.scalar.activation(sumT[0:height, s % 2, :], ps_sum[s % 2][0:height, :], ACT.Copy).then_inc(layer.sumT_ready, 1)

            def total1(g, s):
                act.wait_ge(one.product, g + 1)
                product = ps_out[s % 2][:, 0:GT * (D + 1)].rearrange("p (t d) -> p t d", t=GT)
                nc.scalar.activation(count_all[:, bass.ts(g, GT)], product[:, :, D], ACT.Copy)
                nc.scalar.activation(tot_all[:, bass.ts(g, GT * D)].rearrange("p (t d) -> p t d", t=GT), product[:, :, 0:D],
                                     ACT.Copy).then_inc(one.tot_ready, 1)

            def stage(layer, rows, g, o, places):
                act.wait_ge(layer.tot_ready, g + 1)
                act.wait_ge(one.row_ready, g + 1)
                wait(act, layer.added, (g - places + 1) * (16 * GT))
                nc.scalar.activation(row[:, o, :], rows[:, bass.ts(g, GT)], ACT.Copy)
                nc.scalar.activation(tot[:, o, :], tot_all[:, bass.ts(g, GT * D)], ACT.Copy).then_inc(layer.staged, 1)

            def stage_some(layer, rows, k, s, ahead, beside):
                for q in range(beside):
                    stage(layer, rows, k * beside + (q + beside * (2 - ahead)), beside * ((s + 2) % SLOTS) + q, SLOTS * beside)

            def stage_rest(layer, rows, ahead, beside):
                steps(act, beside * (NG - ahead), NG, lambda g, o, n: stage(layer, rows, g, o, SLOTS * beside),
                      turn=SLOTS * beside)

            def place_x(c, s, n):
                act.wait_ge(x_loaded[s], (n + 1) * 16)
                wait(act, table_stored[s], n * 16)
                nc.scalar.activation(node_rows[:, s, :, 0, :], x_rows[:, s, :, :], ACT.Copy).then_inc(x_placed, 1)
                act.wait_ge(x_placed, c + 1)
                act.dma_start(table_v[:, bass.ts(c, CHUNK * 2 * D)], node_rows[:, s, :, :, :].rearrange("p r k d -> p (r k d)"))\
                    .then_inc(table_stored[s], 16)

            def group1(g, s, n, with_x, with_stage):
                square(one, g, s, GT)
                root(one, g, s, GT)
                if with_x:
                    place_x(g, s, n)
                if begun(g):
                    sums(one, g - 1, (s - 1) % SLOTS, D + 1)
                if begun(g, 2):
                    total1(g - 2, (s - 2) % SLOTS)
                if with_stage:
                    stage_some(one, sum_row_all, g, s, AHEAD1, BESIDE1)

            act.wait_ge(bias_filled, SLOTS)
            phases(act, group1, (0, NC), (AHEAD1 - 2, NG - 2), cut=AHEAD1)
            total1(NG - 2, (NG - 2) % SLOTS)
            sums(one, NG - 1, (NG - 1) % SLOTS, D + 1)
            total1(NG - 1, (NG - 1) % SLOTS)
            stage_rest(one, sum_row_all, AHEAD1, BESIDE1)

            def group2(g, s, n, with_rows, with_stage):
                square(two, g, s, 2 * GT)
                root(two, g, s, 2 * GT)
                act.wait_ge(transposed, g + 1)
                nc.scalar.activation(catT[:, :], ps_catT[:, :], ACT.Copy).then_inc(catT_ready, 1)
                if begun(g):
                    sums(two, g - 1, (s - 1) % SLOTS, P)
                act.wait_ge(hidden, g + 1)
                nc.scalar.activation(hid[:, :, :].rearrange("p t d -> p (t d)"), ps_hid[:, :], ACT.Relu).then_inc(hid_ready, 1)
                if with_rows:
                    store_out(g, s, n)
                if with_stage:
                    stage_some(two, row_all, g, s, AHEAD2, BESIDE2)

            def store_out(c, s, n):
                act.wait_ge(out_ready, c + 1)
                act.dma_start(out_v[:, bass.ts(c, CHUNK * D)], x_rows[:, s, :, :].rearrange("p r d -> p (r d)"))\
                    .then_inc(out_stored[s], 16)

            phases(act, group2, (0, NC), (AHEAD2 - 2, NG - 2), cut=AHEAD2)
            sums(two, NG - 1, (NG - 1) % SLOTS, P)
            stage_rest(two, row_all, AHEAD2, BESIDE2)

        @block.tensor
        def _(pe):
            pe.wait_ge(masks, 4)
            pe.wait_ge(consts_set, 4)
            pe.wait_ge(consts_loaded, 64)
            pe.wait_ge(w_loaded, 16)

            def tile(t, width=P):
                return slice(t * width, (t + 1) * width)

            def node_sums(layer, g, s, left, height):
                for t in range(GT):
                    last = nc.tensor.matmul(ps_sum[s % 2][0:height, :], left[:, t, :], same[:, s % 2, t, :],
                                            start=t == 0, stop=t == GT - 1)
                last.then_inc(layer.summed, 1)

            def product(layer, g, s, right, height, width):
                pe.wait_ge(layer.sumT_ready, g + 1)
                wait(pe, layer.tot_ready, g - 1)
                for t in range(GT):
                    last = nc.tensor.matmul(ps_out[s % 2][:, tile(t, width)], sumT[0:height, s % 2, tile(t)], right,
                                            start=True, stop=True)
                last.then_inc(layer.product, 1)

            def group1(g, s, n):
                pe.wait_ge(one.h_ready, g + 1)
                node_sums(one, g, s, wh[:, s, :, :], D + 1)
                if begun(g):
                    product(one, g - 1, (s - 1) % SLOTS, w_sb[:, :], D + 1, D + 1)

            steps(pe, 0, NG, group1)
            product(one, NG - 1, (NG - 1) % SLOTS, w_sb[:, :], D + 1, D + 1)

            def group2(g, s, n):
                pe.wait_ge(two.h_ready, g + 1)
                for t in range(GT):
                    last = nc.tensor.transpose(ps_catT[:, tile(t)], cat[:, s, t, :], ident[:, :])
                last.then_inc(transposed, 1)
                pe.wait_ge(catT_ready, g + 1)
                for t in range(GT):
                    nc.tensor.matmul(ps_hid[:, tile(t)], catT[:, tile(t)], w1_sb[:, :], start=True, stop=False)
                    last = nc.tensor.matmul(ps_hid[:, tile(t)], ones[:, :], b1_sb[:, :], start=False, stop=True)
                last.then_inc(hidden, 1)
                if begun(g):
                    product(two, g - 1, (s - 1) % SLOTS, w2_sb[:, :], HID, D)
                pe.wait_ge(hid_ready, g + 1)
                node_sums(two, g, s, hid, P)

            steps(pe, 0, NG, group2)
            product(two, NG - 1, (NG - 1) % SLOTS, w2_sb[:, :], HID, D)


def kernel(x, src, dst, edge_attr_32, edge_weight, L0_gnn_w, L0_gnn_b, L1_gnn_W1, L1_gnn_b1, L1_gnn_W2, L1_gnn_b2):
    import numpy as np
    import concourse.bacc as bacc
    from concourse.bass_utils import run_bass_kernel_spmd

    pad = NG * GE - E

    def tiles(a, fill):
        a = np.asarray(a)
        a = np.concatenate([a, np.full((pad,) + a.shape[1:], fill, a.dtype)])
        return np.ascontiguousarray(a.reshape((NG * GT, P) + a.shape[1:]).swapaxes(0, 1))

    src_t, dst_t = (tiles(a, fill).reshape(P, NG, GT) for a, fill in ((src, 0), (dst, N)))
    arrays = {
        "x": np.concatenate([np.asarray(x), np.zeros((NPAD - N, D), np.float32)]),
        "ids": np.ascontiguousarray(np.stack([src_t, dst_t], 2)).reshape(P, NG * 2 * GT),
        "dst_rows": np.concatenate([np.asarray(dst), np.full(pad, N, np.asarray(dst).dtype)]),
        "ew": tiles(edge_weight, 0),
        "ea": tiles(edge_attr_32, 0),
        "w": np.asarray(L0_gnn_w), "b": np.asarray(L0_gnn_b),
        "w1": np.asarray(L1_gnn_W1), "b1": np.asarray(L1_gnn_b1),
        "w2": np.asarray(L1_gnn_W2), "b2": np.asarray(L1_gnn_b2),
    }
    nc = bacc.Bacc("TRN2", target_bir_lowering=False, num_devices=1)
    args = {k: nc.dram_tensor(f"in_{k}", a.shape, mybir.dt.from_np(a.dtype), kind="ExternalInput").ap()
            for k, a in arrays.items()}
    out = nc.dram_tensor("out_rows", (TABLE, D), mybir.dt.float32, kind="ExternalOutput").ap()
    gnn_kernel(nc, **args, out=out)
    r = run_bass_kernel_spmd(nc, [{f"in_{k}": a for k, a in arrays.items()}], core_ids=[0])
    return r.results[0]["out_rows"][:N]
```

```python
import concourse.bass as bass
from concourse import mybir
from contextlib import ExitStack

N, D, E = 100000, 48, 25000
DE, HID = 32, 128
P = 128
GT = 4
GE = GT * P
NG = -(-E // GE)
SLOTS = 4
AHEAD1, AHEAD2 = 24, 32
BESIDE1, BESIDE2 = 2, 3
LAG = 4
ONE1, ONE2 = ((ahead * beside - LAG) // (beside - 1) for ahead, beside in ((AHEAD1, BESIDE1), (AHEAD2, BESIDE2)))
CHUNK = 28
ROWS = -(-N // (P * CHUNK)) * CHUNK
NPAD = ROWS * P
SPARE = GE
TABLE = NPAD + SPARE
NC = ROWS // CHUNK
PART = 14
PARTS = ROWS // PART
FILLS = 20
COPY_FROM = NG - PARTS // 2
EPS = 1e-5


def gnn_kernel(nc, x, ids, dst_rows, ew, ea, w, b, w1, b1, w2, b2, out):
    f32, i32 = mybir.dt.float32, mybir.dt.int32
    ALU, ACT, AX = mybir.AluOpType, mybir.ActivationFunctionType, mybir.AxisListType
    assert ROWS % PART == 0 and PARTS % 2 == 0 and 2 * FILLS <= PARTS <= 3 * FILLS and COPY_FROM >= 0
    assert FILLS <= AHEAD1 - 4 and NC <= AHEAD2 - 4 and AHEAD1 % SLOTS == AHEAD2 % SLOTS == 0
    for ahead, beside, one_beside in (AHEAD1, BESIDE1, ONE1), (AHEAD2, BESIDE2, ONE2):
        assert one_beside <= NG and beside * (one_beside - ahead) == one_beside - LAG

    table = nc.dram_tensor("table", (TABLE, 2 * D), f32, kind="Internal").ap()
    table_parts = table.rearrange("n (k d) -> (n k) d", k=2)

    x_v = x.rearrange("(p r) d -> p r d", p=P)
    table_halves = table[0:NPAD, :].rearrange("(p r) (k d) -> p r k d", p=P, k=2)
    table_v = table[0:NPAD, :].rearrange("(p r) d -> p (r d)", p=P)
    table_spare = table[NPAD:TABLE, :].rearrange("(p r) d -> p (r d)", p=P)
    out_v = out[0:NPAD, :].rearrange("(p r) d -> p (r d)", p=P)
    out_spare = out[NPAD:TABLE, :].rearrange("(p r) d -> p (r d)", p=P)

    with ExitStack() as ctx:
        def sb(name, shape, dt=f32):
            return ctx.enter_context(nc.sbuf_tensor(name, shape, dt))

        def sem(name):
            return ctx.enter_context(nc.semaphore(name))

        def slot_sems(name):
            return [sem(f"{name}{s}") for s in range(SLOTS)]

        ident = sb("ident", [P, P])
        earlier = sb("earlier", [P, P])
        spare_i = sb("spare_i", [P, GT], i32)
        spare = sb("spare", [P, GT])
        w_sb = sb("w_sb", [D + 1, D + 1])
        w1_sb = sb("w1_sb", [P, HID])
        w2_sb = sb("w2_sb", [HID, D])
        b1_sb = sb("b1_sb", [1, HID])
        ones = sb("ones", [1, P])
        b_sb = sb("b_sb", [P, D])
        b2_sb = sb("b2_sb", [P, D])
        eps = sb("eps", [P, 1])
        sum_row_all = sb("sum_row_all", [P, NG * GT], i32)
        row_all = sb("row_all", [P, NG * GT], i32)
        tot_all = sb("tot_all", [P, NG * GT * D])
        count_all = sb("count_all", [P, NG * GT])
        idx = sb("idx", [P, SLOTS, 2 * GT], i32)
        weight = sb("weight", [P, SLOTS, GT])
        dst_line = sb("dst_line", [1, SLOTS, GE], i32)
        dst_row = sb("dst_row", [P, SLOTS, GE], i32)
        dst_col = sb("dst_col", [P, SLOTS, GT])
        raw1 = sb("raw1", [P, SLOTS, GT, D])
        raw2 = sb("raw2", [P, SLOTS, GT, 2, 2 * D])
        x1 = sb("x1", [P, SLOTS, 2 * GT, D])
        cat = sb("cat", [P, SLOTS, GT, 2 * D + DE])
        same = sb("same", [P, 2, GT, GE])
        wh = sb("wh", [P, SLOTS, GT, D + 1])
        xc = sb("xc", [P, SLOTS, 2 * GT, D])
        sq = sb("sq", [P, SLOTS, 2 * GT, D])
        var = sb("var", [P, SLOTS, 2 * GT])
        std = sb("std", [P, SLOTS, 2 * GT])
        sumT = sb("sumT", [P, 2, GE])
        row = sb("row", [P, SLOTS * max(BESIDE1, BESIDE2), GT], i32)
        tot = sb("tot", [P, SLOTS * max(BESIDE1, BESIDE2), GT * D])
        scratch = sb("scratch", [P, GT, P], mybir.dt.bfloat16)
        scalar_scratch = sb("scalar_scratch", [P, sum(range(GT)) * P], mybir.dt.bfloat16)
        n_tile = sb("n_tile", [P, GT])
        n_tiles = sb("n_tiles", [P, GT])
        n_before = sb("n_before", [P, GT])
        offset = sb("offset", [P, GT])
        lead = sb("lead", [P, GT])
        row_f = sb("row_f", [P, GT])
        total = sb("total", [P, 2 * GT])
        rstd = sb("rstd", [P, 2 * GT])
        scale = sb("scale", [P, GT])
        bias2 = sb("bias2", [P, SLOTS, GT, D])
        catT = sb("catT", [P, GE])
        hid = sb("hid", [P, GT, HID])
        node_rows = sb("node_rows", [P, SLOTS, CHUNK, 2, D])
        x_rows = sb("x_rows", [P, SLOTS, CHUNK, D])
        bias_rows = node_rows[:, 0, :, :, :].rearrange("p r k d -> p (r k) d")[:, 0:PART, :]
        zero = node_rows[:, 1, :, :, :].rearrange("p r k d -> p (r k d)")[:, 0:SPARE // P * 2 * D]

        def bank(name):
            return ctx.enter_context(nc.psum_tensor(name, [P, GE], f32))

        ps_sum = [bank(f"ps_sum{s}") for s in range(2)]
        ps_out = [bank(f"ps_out{s}") for s in range(2)]
        ps_catT = bank("ps_catT")
        ps_hid = bank("ps_hid")

        masks, masks_ready, spare_ready = sem("masks"), sem("masks_ready"), sem("spare_ready")
        consts_loaded, w_loaded, bias_loaded = sem("consts_loaded"), sem("w_loaded"), sem("bias_loaded")
        consts_set, bias_filled = sem("consts_set"), sem("bias_filled")
        zero_ready, spare_stored = sem("zero_ready"), sem("spare_stored")
        vector_step = sem("vector_step")

        dst_spread = sem("dst_spread")
        compared = sem("compared")
        pool_turns = sem("pool_turns")

        class Layer:
            def __init__(self, n):
                self.loaded = slot_sems(f"loaded{n}_")
                self.gathered = slot_sems(f"gathered{n}_")
                self.added = sem(f"added{n}")
                self.centred = sem(f"centred{n}")
                self.squared = sem(f"squared{n}")
                self.var_ready = sem(f"var_ready{n}")
                self.std_ready = sem(f"std_ready{n}")
                self.row_ready = sem(f"row_ready{n}")
                self.h_ready = sem(f"h_ready{n}")
                self.summed = sem(f"summed{n}")
                self.sumT_ready = sem(f"sumT_ready{n}")
                self.product = sem(f"product{n}")
                self.tot_ready = sem(f"tot_ready{n}")
                self.staged = sem(f"staged{n}")

        one, two = Layer(1), Layer(2)
        transposed, catT_ready = sem("transposed"), sem("catT_ready")
        hidden, hid_ready = sem("hidden"), sem("hid_ready")
        sums_begun, x_copied = sem("sums_begun"), sem("x_copied")
        rows_loaded, out_stored = slot_sems("rows_loaded"), slot_sems("out_stored")
        out_ready = sem("out_ready")

        def wait(eng, s, value):
            if not isinstance(value, int) or value > 0:
                eng.wait_ge(s, value)

        def steps(eng, start, end, body, turn=SLOTS):
            first = min(end, (start // turn + 1) * turn)
            turns = max(0, end - first) // turn
            for k in range(start, first):
                body(k, k % turn, k // turn)
            if turns:
                with eng.Fori(first // turn, first // turn + turns) as i:
                    for s in range(turn):
                        body(i * turn + s, s, i)
            for k in range(first + turns * turn, end):
                body(k, k % turn, k // turn)

        def phases(eng, body, *flags):
            cuts = sorted({0, NG, *(c for f in flags for c in f)})
            for a, z in zip(cuts, cuts[1:]):
                on = [f[0] <= a < f[1] for f in flags]
                steps(eng, a, z, lambda k, s, n: body(k, s, n, *on))

        def begun(g, back=1):
            return not isinstance(g, int) or g >= back

        block = ctx.enter_context(nc.Block())

        @block.sync
        def _(sp):
            sp.dma_start(b_sb[:, :], b.partition_broadcast(P)).then_inc(bias_loaded, 16)

            def load1(g, s, n, for_spread=True):
                wait(sp, one.h_ready, g - SLOTS + 1)
                sp.dma_start(idx[:, s, :], ids[:, bass.ts(g, 2 * GT)]).then_inc(one.loaded[s], 16)
                if for_spread:
                    sp.dma_start(dst_line[:, s, :], dst_rows[bass.ts(g, GE)].rearrange("(a n) -> a n", a=1)).then_inc(one.loaded[s], 16)
                else:
                    sp.dma_start(dst_row[:, s, :], dst_rows[bass.ts(g, GE)].partition_broadcast(P)).then_inc(one.loaded[s], 16)
                sp.dma_start(weight[:, s, :], ew[:, bass.ts(g, GT)]).then_inc(one.loaded[s], 16)

            for g in range(SLOTS):
                load1(g, g, 0)
            sp.dma_start(b2_sb[:, :], b2.partition_broadcast(P)).then_inc(consts_loaded, 16)
            sp.dma_start(w1_sb[:, :], w1).then_inc(consts_loaded, 16)
            sp.dma_start(w2_sb[:, :], w2).then_inc(consts_loaded, 16)
            sp.dma_start(b1_sb[:, :], b1.rearrange("(a n) -> a n", a=1)).then_inc(consts_loaded, 16)
            sp.wait_ge(masks_ready, 1)
            sp.dma_start(w_sb[0:D, 0:D], w).then_inc(w_loaded, 16)
            steps(sp, SLOTS, FILLS, load1)
            steps(sp, FILLS, NG, lambda g, s, n: load1(g, s, n, False))

            def load2(g, s, n):
                wait(sp, two.h_ready, g - SLOTS + 1)
                wait(sp, transposed, g - SLOTS + 1)
                sp.dma_start(idx[:, s, :], ids[:, bass.ts(g, 2 * GT)]).then_inc(two.loaded[s], 16)
                sp.dma_start(dst_row[:, s, :], dst_rows[bass.ts(g, GE)].partition_broadcast(P)).then_inc(two.loaded[s], 16)
                sp.dma_start(cat[:, s, :, 2 * D:], ea[:, bass.ts(g, GT), :]).then_inc(two.loaded[s], 16)

            def load_rows(c, s, n):
                wait(sp, out_ready, c - SLOTS + 1)
                sp.dma_start(node_rows[:, s, :, :, :].rearrange("p r k d -> p (r k d)"),
                             table_v[:, bass.ts(c, CHUNK * 2 * D)]).then_inc(rows_loaded[s], 16)

            def load2_rows(g, s, n):
                load2(g, s, n)
                load_rows(g, s, n)

            sp.wait_ge(one.h_ready, NG)
            for g in range(SLOTS):
                load2(g, g, 0)
            sp.wait_ge(x_copied, 16 * PARTS)
            sp.wait_ge(one.added, 16 * GT * NG)
            for g in range(SLOTS):
                load_rows(g, g, 0)
            steps(sp, SLOTS, NC, load2_rows)
            steps(sp, NC, NG, load2)
            sp.wait_ge(two.added, 16 * GT * NG)
            for s in range(SLOTS):
                sp.wait_ge(out_stored[s], 16 * len(range(s, NC, SLOTS)))
            sp.wait_ge(spare_stored, 32)

        @block.gpsimd
        def _(pool):
            nc.gpsimd.memset(ident[:, :], 0.0).then_inc(masks, 1)
            nc.gpsimd.memset(earlier[:, :], 1.0).then_inc(masks, 1)
            pool.wait_ge(masks, 2)
            nc.gpsimd.affine_select(out=ident[:, :], in_=ident[:, :], compare_op=ALU.not_equal, fill=1.0,
                                    base=0, pattern=[[-1, P]], channel_multiplier=1).then_inc(masks, 1)
            nc.gpsimd.affine_select(out=earlier[:, :], in_=earlier[:, :], compare_op=ALU.is_gt, fill=0.0,
                                    base=0, pattern=[[-1, P]], channel_multiplier=1).then_inc(masks, 1)
            pool.wait_ge(masks, 4)
            nc.gpsimd.tensor_copy(w_sb[:, :], ident[0:D + 1, 0:D + 1]).then_inc(masks_ready, 1)
            nc.gpsimd.iota(spare_i[:, :], pattern=[[P, GT]], base=NPAD, channel_multiplier=1).then_inc(spare_ready, 1)

            def gather(source, to, s, column, done):
                pool.indirect_dma_start(to, None, source, bass.IndirectOffsetOnAxis(ap=idx[:, s, column:column + 1], axis=0),
                                        bounds_check=NPAD - 1, oob_is_err=False).then_inc(done, 16)

            def gather1(g, s, n, tiles, spread=False):
                pool.wait_ge(one.loaded[s], 48 * (n + 1))
                pool.sem_inc(pool_turns, 1)
                for t in tiles:
                    gather(x, raw1[:, s, t, :], s, t, one.gathered[s])
                if spread:
                    nc.gpsimd.partition_broadcast(dst_row[:, s, :], dst_line[:, s, :]).then_inc(dst_spread, 1)

            def gather2(g, s, n, tiles):
                pool.wait_ge(two.loaded[s], 48 * (n + 1))
                pool.sem_inc(pool_turns, 1)
                for t in tiles:
                    gather(table, raw2[:, s, t, 0, :], s, GT + t, two.gathered[s])
                    gather(table, raw2[:, s, t, 1, :], s, t, two.gathered[s])

            def add(to, layer, g, o):
                pool.wait_ge(layer.staged, g + 1)
                wait(pool, layer.added, g * (16 * GT))
                pool.sem_inc(pool_turns, 1)
                for t in range(GT):
                    pool.indirect_dma_start(to, bass.IndirectOffsetOnAxis(ap=row[:, o, t:t + 1], axis=0),
                                            tot[:, o, t * D:(t + 1) * D], None, compute_op=ALU.add).then_inc(layer.added, 16)

            def run_layer(to, layer, gather_group, spread, ahead, beside, one_beside, start_ready):
                steps(pool, 0, spread, lambda g, s, n: gather_group(g, s, n, range(GT), spread=True))
                steps(pool, spread, ahead, lambda g, s, n: gather_group(g, s, n, range(GT)))
                start_ready()

                def gather_and_add(k, s, n):
                    for q in range(beside):
                        gather_group(k, s, n, range(q * GT // beside, (q + 1) * GT // beside))
                        add(to, layer, k * beside + (q - beside * ahead), beside * ((s - ahead) % SLOTS) + q)

                steps(pool, ahead, one_beside, gather_and_add)

                def gather_and_add_one(k, s, n):
                    gather_group(k, s, n, range(GT))
                    add(to, layer, k - LAG, beside * ((s - ahead) % SLOTS))

                steps(pool, one_beside, NG, gather_and_add_one)
                for k in range(NG, NG + LAG):
                    add(to, layer, k - LAG, beside * ((k - ahead) % SLOTS))

            def table_ready():
                pool.wait_ge(sums_begun, 16 * PARTS)
                pool.wait_ge(spare_stored, 32)

            def out_started():
                for s in range(SLOTS):
                    pool.wait_ge(out_stored[s], 16 * len(range(s, NC, SLOTS)))

            run_layer(table_parts, one, gather1, FILLS, AHEAD1, BESIDE1, ONE1, table_ready)
            pool.wait_ge(one.added, 16 * GT * NG)
            pool.wait_ge(x_copied, 16 * PARTS)
            run_layer(out, two, gather2, 0, AHEAD2, BESIDE2, ONE2, out_started)

        @block.vector
        def _(dve):
            nc.vector.memset(ones[:, :], 1.0).then_inc(consts_set, 1)
            nc.vector.memset(eps[:, :], EPS).then_inc(consts_set, 1)
            nc.vector.memset(n_tiles[:, 0:1], 0.0).then_inc(consts_set, 1)
            nc.vector.memset(wh[:, :, :, D:D + 1], 1.0).then_inc(consts_set, 1)
            nc.vector.memset(zero, 0.0).then_inc(zero_ready, 1)
            dve.wait_ge(bias_loaded, 16)
            nc.vector.tensor_copy(bias_rows, b_sb[:, :].unsqueeze(1).broadcast_to([P, PART, D])).then_inc(bias_filled, 1)
            dve.wait_ge(spare_ready, 1)
            nc.vector.tensor_copy(spare[:, :], spare_i[:, :]).then_inc(consts_set, 1)
            dve.wait_ge(consts_set, 5)
            dve.wait_ge(masks, 4)

            def over_features(a):
                return a.unsqueeze(2).broadcast_to([P, a.shape[1], D])

            def chain(base):
                count = [0]

                def passed(*instructions):
                    for instruction in instructions:
                        instruction.then_inc(vector_step, 1)
                    count[0] += len(instructions)
                    dve.wait_ge(vector_step, base + count[0])
                return passed, count

            def compare(s):
                for t in range(GT):
                    last = nc.vector.tensor_scalar(same[:, s % 2, t, :], dst_row[:, s, :], dst_col[:, s, t:t + 1], None, ALU.is_equal)
                return last

            def total_of(rows):
                return nc.vector.tensor_reduce(total[:, 0:rows.shape[1]], rows, AX.X, ALU.add)

            def centre(layer, s, rows):
                count = rows.shape[1]
                nc.vector.scalar_tensor_tensor(out=xc[:, s, 0:count, :], in0=over_features(total[:, 0:count]), scalar=-1.0 / D,
                                               in1=rows, op0=ALU.mult, op1=ALU.add).then_inc(layer.centred, 1)

            STEPS1 = 9

            def group1(g, s, n, spread):
                passed, count = chain(g * STEPS1)
                dve.wait_ge(one.loaded[s], 48 * (n + 1))
                own = nc.vector.tensor_copy(dst_col[:, s, :], idx[:, s, GT:2 * GT])
                dve.wait_ge(one.gathered[s], 16 * GT * (n + 1))
                passed(own, total_of(raw1[:, s, :, :]))
                centre(one, s, raw1[:, s, :, :])
                away = nc.vector.tensor_tensor(offset[:, :], dst_col[:, s, :], spare[:, :], ALU.subtract)
                if spread:
                    dve.wait_ge(dst_spread, g + 1)
                wait(dve, one.summed, g - 1)
                compare(s).then_inc(compared, 1)
                for t in range(GT):
                    last = nc.vector.scalar_tensor_tensor(
                        out=scratch[:, t, :], in0=dst_row[:, s, t * P:(t + 1) * P], scalar=dst_col[:, s, t:t + 1],
                        in1=earlier[:, :], op0=ALU.is_equal, op1=ALU.mult, accum_out=n_tile[:, t:t + 1])
                dve.wait_ge(one.squared, g + 1)
                nc.vector.tensor_reduce(var[:, s, 0:GT], sq[:, s, 0:GT, :], AX.X, ALU.add).then_inc(one.var_ready, 1)
                dve.wait_ge(one.std_ready, g + 1)
                passed(away, last)
                passed(nc.vector.tensor_tensor(n_before[:, :], n_tile[:, :], n_tiles[:, :], ALU.add),
                       nc.vector.reciprocal(rstd[:, 0:GT], std[:, s, 0:GT]))
                passed(nc.vector.scalar_tensor_tensor(out=lead[:, :], in0=n_before[:, :], scalar=0.0, in1=offset[:, :],
                                                      op0=ALU.is_equal, op1=ALU.mult))
                passed(nc.vector.tensor_tensor(scale[:, :], rstd[:, 0:GT], weight[:, s, :], ALU.mult),
                       nc.vector.tensor_tensor(row_f[:, :], lead[:, :], spare[:, :], ALU.add))
                nc.vector.scalar_tensor_tensor(out=wh[:, s, :, 0:D], in0=xc[:, s, 0:GT, :], scalar=0.0,
                                               in1=over_features(scale[:, :]), op0=ALU.max, op1=ALU.mult).then_inc(one.h_ready, 1)
                nc.vector.tensor_copy(row_all[:, bass.ts(g, GT)], row_f[:, :])
                nc.vector.tensor_scalar(sum_row_all[:, bass.ts(g, GT)], row_f[:, :], 2.0, 1.0, ALU.mult, ALU.add)\
                    .then_inc(one.row_ready, 1)
                assert count[0] == STEPS1, count

            phases(dve, group1, (0, FILLS))

            dve.wait_ge(consts_loaded, 64)

            def total2(g, s, passed):
                passed(nc.vector.tensor_tensor(bias2[:, s, :, :], b2_sb[:, :].unsqueeze(1).broadcast_to([P, GT, D]),
                                             over_features(count_all[:, bass.ts(g, GT)]), ALU.mult))
                dve.wait_ge(two.product, g + 1)
                nc.vector.tensor_tensor(tot_all[:, bass.ts(g, GT * D)], ps_out[s % 2][:, 0:GT * D],
                                        bias2[:, s, :, :].rearrange("p t d -> p (t d)"), ALU.add).then_inc(two.tot_ready, 1)

            STEPS2 = 5

            def group2(g, s, n):
                passed, count = chain(g * STEPS2 + NG * STEPS1)
                dve.wait_ge(two.loaded[s], 48 * (n + 1))
                own = nc.vector.tensor_copy(dst_col[:, s, :], idx[:, s, GT:2 * GT])
                dve.wait_ge(two.gathered[s], 32 * GT * (n + 1))
                parts = raw2[:, s, :, :, :].rearrange("p t k d -> p (t k) d")
                passed(own, nc.vector.scalar_tensor_tensor(out=x1[:, s, :, :], in0=parts[:, :, D:2 * D], scalar=0.0,
                                                           in1=parts[:, :, 0:D], op0=ALU.max, op1=ALU.add))
                passed(total_of(x1[:, s, :, :]))
                centre(two, s, x1[:, s, :, :])
                wait(dve, two.summed, g - 1)
                compare(s)
                dve.wait_ge(two.squared, g + 1)
                nc.vector.tensor_reduce(var[:, s, :], sq[:, s, :, :], AX.X, ALU.add).then_inc(two.var_ready, 1)
                if begun(g, 2):
                    total2(g - 2, (s - 2) % SLOTS, passed)
                else:
                    passed(nc.vector.memset(scratch[:, 0:1], 0.0))
                dve.wait_ge(two.std_ready, g + 1)
                passed(nc.vector.reciprocal(rstd[:, :], std[:, s, :]))
                for k in range(2):
                    scales = rstd[:, :].rearrange("p (t k) -> p k t", k=2)[:, k, :]
                    last = nc.vector.scalar_tensor_tensor(
                        out=cat[:, s, :, k * D:(k + 1) * D], in0=xc[:, s, :, :].rearrange("p (t k) d -> p k t d", k=2)[:, k, :, :],
                        scalar=0.0, in1=over_features(scales), op0=ALU.max, op1=ALU.mult)
                last.then_inc(two.h_ready, 1)
                assert count[0] == STEPS2, count

            def start_out(c, s, n):
                dve.wait_ge(rows_loaded[s], (n + 1) * 16)
                wait(dve, out_stored[s], n * 16)
                nc.vector.scalar_tensor_tensor(out=x_rows[:, s, :, :], in0=node_rows[:, s, :, 1, :], scalar=0.0,
                                               in1=node_rows[:, s, :, 0, :], op0=ALU.max, op1=ALU.add).then_inc(out_ready, 1)

            def group2_rows(g, s, n, with_rows):
                group2(g, s, n)
                if with_rows:
                    start_out(g, s, n)

            phases(dve, group2_rows, (0, NC))
            passed, _ = chain(NG * (STEPS1 + STEPS2))
            for g in (NG - 2, NG - 1):
                total2(g, g % SLOTS, passed)

        @block.scalar
        def _(act):
            act.wait_ge(zero_ready, 1)
            act.dma_start(out_spare, zero[:, 0:SPARE // P * D]).then_inc(spare_stored, 16)
            act.dma_start(table_spare, zero).then_inc(spare_stored, 16)
            act.wait_ge(consts_set, 5)

            def square(layer, g, s, count):
                act.wait_ge(layer.centred, g + 1)
                nc.scalar.activation(sq[:, s, 0:count, :], xc[:, s, 0:count, :], ACT.Square).then_inc(layer.squared, 1)

            def root(layer, g, s, count):
                act.wait_ge(layer.var_ready, g + 1)
                nc.scalar.activation(std[:, s, 0:count], var[:, s, 0:count], ACT.Sqrt, scale=1.0 / D, bias=eps[:, :])\
                    .then_inc(layer.std_ready, 1)

            def sums(layer, g, s, height):
                act.wait_ge(layer.summed, g + 1)
                wait(act, layer.product, g - 1)
                nc.scalar.activation(sumT[0:height, s % 2, :], ps_sum[s % 2][0:height, :], ACT.Copy).then_inc(layer.sumT_ready, 1)

            def total1(g, s):
                act.wait_ge(one.product, g + 1)
                product = ps_out[s % 2][:, 0:GT * (D + 1)].rearrange("p (t d) -> p t d", t=GT)
                nc.scalar.activation(count_all[:, bass.ts(g, GT)], product[:, :, D], ACT.Copy)
                nc.scalar.activation(tot_all[:, bass.ts(g, GT * D)].rearrange("p (t d) -> p t d", t=GT), product[:, :, 0:D],
                                     ACT.Copy).then_inc(one.tot_ready, 1)

            def stage(layer, rows, g, o, places):
                act.wait_ge(layer.tot_ready, g + 1)
                act.wait_ge(one.row_ready, g + 1)
                wait(act, layer.added, (g - places + 1) * (16 * GT))
                nc.scalar.activation(row[:, o, :], rows[:, bass.ts(g, GT)], ACT.Copy)
                nc.scalar.activation(tot[:, o, :], tot_all[:, bass.ts(g, GT * D)], ACT.Copy).then_inc(layer.staged, 1)

            def stage_some(layer, rows, k, s, ahead, beside):
                for q in range(beside):
                    stage(layer, rows, k * beside + (q - beside * ahead), beside * ((s - ahead) % SLOTS) + q, SLOTS * beside)

            def stage_one(layer, rows, k, s, ahead, beside):
                stage(layer, rows, k - LAG, beside * ((s - ahead) % SLOTS), SLOTS)

            def begin_sums(c):
                act.dma_start(table_halves[:, bass.ts(c, PART), 1, :], bias_rows).then_inc(sums_begun, 16)

            def copy_x(c):
                act.dma_start(table_halves[:, bass.ts(c, PART), 0, :], x_v[:, bass.ts(c, PART), :]).then_inc(x_copied, 16)

            def group1(g, s, n, with_sums, with_third, with_x, with_first, with_more, with_one):
                square(one, g, s, GT)
                act.wait_ge(compared, g + 1)
                for t in range(1, GT):
                    nc.scalar.activation(scalar_scratch[:, t * (t - 1) // 2 * P:t * (t + 1) // 2 * P], same[:, s % 2, t, 0:t * P],
                                         ACT.Copy, accum_out=n_tiles[:, t:t + 1])
                root(one, g, s, GT)
                if with_sums:
                    begin_sums(g * 2)
                    begin_sums(g * 2 + 1)
                if with_third:
                    begin_sums(g + 2 * FILLS)
                if with_x:
                    copy_x(g * 2 - COPY_FROM * 2)
                if begun(g):
                    sums(one, g - 1, (s - 1) % SLOTS, D + 1)
                if begun(g, 2):
                    total1(g - 2, (s - 2) % SLOTS)
                if with_x:
                    copy_x(g * 2 - COPY_FROM * 2 + 1)
                if with_first:
                    stage_some(one, sum_row_all, g + 4, s, AHEAD1, BESIDE1)
                if with_more:
                    stage_some(one, sum_row_all, g + 2, s + 2, AHEAD1, BESIDE1)
                if with_one:
                    stage_one(one, sum_row_all, g + 2, s + 2, AHEAD1, BESIDE1)

            act.wait_ge(bias_filled, 1)
            phases(act, group1, (0, FILLS), (0, PARTS - 2 * FILLS), (COPY_FROM, NG),
                   (AHEAD1 - 4, AHEAD1 - 2), (AHEAD1, ONE1 - 2), (ONE1 - 2, NG))
            total1(NG - 2, (NG - 2) % SLOTS)
            stage_one(one, sum_row_all, NG + 2, NG + 2, AHEAD1, BESIDE1)
            sums(one, NG - 1, (NG - 1) % SLOTS, D + 1)
            total1(NG - 1, (NG - 1) % SLOTS)
            stage_one(one, sum_row_all, NG + 3, NG + 3, AHEAD1, BESIDE1)

            def group2(g, s, n, with_rows, with_first, with_more, with_one):
                square(two, g, s, 2 * GT)
                root(two, g, s, 2 * GT)
                act.wait_ge(transposed, g + 1)
                nc.scalar.activation(catT[:, :], ps_catT[:, :], ACT.Copy).then_inc(catT_ready, 1)
                if begun(g):
                    sums(two, g - 1, (s - 1) % SLOTS, P)
                act.wait_ge(hidden, g + 1)
                nc.scalar.activation(hid[:, :, :].rearrange("p t d -> p (t d)"), ps_hid[:, :], ACT.Relu).then_inc(hid_ready, 1)
                if with_rows:
                    store_out(g, s, n)
                if with_first:
                    stage_some(two, row_all, g + 4, s, AHEAD2, BESIDE2)
                if with_more:
                    stage_some(two, row_all, g + 2, s + 2, AHEAD2, BESIDE2)
                if with_one:
                    stage_one(two, row_all, g + 2, s + 2, AHEAD2, BESIDE2)

            def store_out(c, s, n):
                act.wait_ge(out_ready, c + 1)
                act.dma_start(out_v[:, bass.ts(c, CHUNK * D)], x_rows[:, s, :, :].rearrange("p r d -> p (r d)"))\
                    .then_inc(out_stored[s], 16)

            phases(act, group2, (0, NC), (AHEAD2 - 4, AHEAD2 - 2), (AHEAD2, ONE2 - 2), (ONE2 - 2, NG))
            sums(two, NG - 1, (NG - 1) % SLOTS, P)
            for k in (NG + 2, NG + 3):
                stage_one(two, row_all, k, k, AHEAD2, BESIDE2)

        @block.tensor
        def _(pe):
            pe.wait_ge(masks, 4)
            pe.wait_ge(consts_set, 5)
            pe.wait_ge(consts_loaded, 64)
            pe.wait_ge(w_loaded, 16)

            def tile(t, width=P):
                return slice(t * width, (t + 1) * width)

            def node_sums(layer, g, s, left, height):
                for t in range(GT):
                    last = nc.tensor.matmul(ps_sum[s % 2][0:height, :], left[:, t, :], same[:, s % 2, t, :],
                                            start=t == 0, stop=t == GT - 1)
                last.then_inc(layer.summed, 1)

            def product(layer, g, s, right, height, width):
                pe.wait_ge(layer.sumT_ready, g + 1)
                wait(pe, layer.tot_ready, g - 1)
                for t in range(GT):
                    last = nc.tensor.matmul(ps_out[s % 2][:, tile(t, width)], sumT[0:height, s % 2, tile(t)], right,
                                            start=True, stop=True)
                last.then_inc(layer.product, 1)

            def group1(g, s, n):
                pe.wait_ge(one.h_ready, g + 1)
                node_sums(one, g, s, wh[:, s, :, :], D + 1)
                if begun(g):
                    product(one, g - 1, (s - 1) % SLOTS, w_sb[:, :], D + 1, D + 1)

            steps(pe, 0, NG, group1)
            product(one, NG - 1, (NG - 1) % SLOTS, w_sb[:, :], D + 1, D + 1)

            def group2(g, s, n):
                pe.wait_ge(two.h_ready, g + 1)
                for t in range(GT):
                    last = nc.tensor.transpose(ps_catT[:, tile(t)], cat[:, s, t, :], ident[:, :])
                last.then_inc(transposed, 1)
                pe.wait_ge(catT_ready, g + 1)
                for t in range(GT):
                    nc.tensor.matmul(ps_hid[:, tile(t)], catT[:, tile(t)], w1_sb[:, :], start=True, stop=False)
                    last = nc.tensor.matmul(ps_hid[:, tile(t)], ones[:, :], b1_sb[:, :], start=False, stop=True)
                last.then_inc(hidden, 1)
                if begun(g):
                    product(two, g - 1, (s - 1) % SLOTS, w2_sb[:, :], HID, D)
                pe.wait_ge(hid_ready, g + 1)
                node_sums(two, g, s, hid, P)

            steps(pe, 0, NG, group2)
            product(two, NG - 1, (NG - 1) % SLOTS, w2_sb[:, :], HID, D)


def kernel(x, src, dst, edge_attr_32, edge_weight, L0_gnn_w, L0_gnn_b, L1_gnn_W1, L1_gnn_b1, L1_gnn_W2, L1_gnn_b2):
    import numpy as np
    import concourse.bacc as bacc
    from concourse.bass_utils import run_bass_kernel_spmd

    pad = NG * GE - E

    def tiles(a, fill):
        a = np.asarray(a)
        a = np.concatenate([a, np.full((pad,) + a.shape[1:], fill, a.dtype)])
        return np.ascontiguousarray(a.reshape((NG * GT, P) + a.shape[1:]).swapaxes(0, 1))

    src_t, dst_t = (tiles(a, fill).reshape(P, NG, GT) for a, fill in ((src, 0), (dst, N)))
    arrays = {
        "x": np.concatenate([np.asarray(x), np.zeros((NPAD - N, D), np.float32)]),
        "ids": np.ascontiguousarray(np.stack([src_t, dst_t], 2)).reshape(P, NG * 2 * GT),
        "dst_rows": np.concatenate([np.asarray(dst), np.full(pad, N, np.asarray(dst).dtype)]),
        "ew": tiles(edge_weight, 0),
        "ea": tiles(edge_attr_32, 0),
        "w": np.asarray(L0_gnn_w), "b": np.asarray(L0_gnn_b),
        "w1": np.asarray(L1_gnn_W1), "b1": np.asarray(L1_gnn_b1),
        "w2": np.asarray(L1_gnn_W2), "b2": np.asarray(L1_gnn_b2),
    }
    nc = bacc.Bacc("TRN2", target_bir_lowering=False, num_devices=1)
    args = {k: nc.dram_tensor(f"in_{k}", a.shape, mybir.dt.from_np(a.dtype), kind="ExternalInput").ap()
            for k, a in arrays.items()}
    out = nc.dram_tensor("out_rows", (TABLE, D), mybir.dt.float32, kind="ExternalOutput").ap()
    gnn_kernel(nc, **args, out=out)
    r = run_bass_kernel_spmd(nc, [{f"in_{k}": a for k, a in arrays.items()}], core_ids=[0])
    return r.results[0]["out_rows"][:N]
```
